# Optimizing a Trainium2 kernel written in Bass

```python
import numpy as np
import jax
import jax.numpy as jnp

def _softmax(x, axis=-1):
    return jax.nn.softmax(x, axis=axis)

def _gelu(x):
    return jax.nn.gelu(x, approximate=True)

def _silu(x):
    return jax.nn.silu(x)

def _sigmoid(x):
    return jax.nn.sigmoid(x)

def _layernorm(x, axis=-1, eps=1e-05):
    m = jnp.mean(x, axis=axis, keepdims=True)
    v = jnp.var(x, axis=axis, keepdims=True)
    return (x - m) / jnp.sqrt(v + eps)

def _scatter_add(tgt, idx, src, axis=0):
    return tgt.at[idx].add(src)

def _segment_sum(src, seg, n):
    return jax.ops.segment_sum(src, seg, n)
kernel_name = 'mk_gnn_resnorm_d1_gnn_r64_b99fca'

def setup_inputs(seed: int=0):
    np.random.seed(seed)
    _w = jnp.asarray

    def _rec_inputs():
        import jax
        import jax.numpy as jnp
        _gk = jax.random.key(seed)
        x = -0.000202 + 1 * jax.random.normal(jax.random.fold_in(_gk, 1), (100000, 128), jnp.float32)
        src = jax.random.randint(jax.random.fold_in(_gk, 2), (25000,), 0, 100000, jnp.int32)
        dst = jnp.minimum((100000 * jax.random.uniform(jax.random.fold_in(_gk, 3), (25000,)) ** 2.0).astype(jnp.int32), 99999)
        _o = jnp.argsort(dst, stable=True)
        src = src[_o]
        dst = dst[_o]
        edge_attr_128 = -5.16925e-05 + 1.00005 * jax.random.normal(jax.random.fold_in(_gk, 11), (25000, 128), jnp.float32)
        edge_weight1 = jax.random.uniform(jax.random.fold_in(_gk, 13), (25000, 1), jnp.float32, 0.0, 0.999999)
        return (x, src, dst, edge_attr_128, edge_weight1)
    x, src, dst, edge_attr_128, edge_weight1 = _rec_inputs()

    def _L0_gnn_setup():
        import jax, jax.numpy as jnp
        import numpy as np
        N_NODES = 50000
        N_EDGES = 12500
        IN_CH = 128
        OUT_CH = 128
        EDGE_DIM = 128
        key = jax.random.key(seed)
        ks = jax.random.split(key, 10)
        x = jax.random.normal(ks[0], (N_NODES, IN_CH), dtype=jnp.float32)
        edge_index = jax.random.randint(ks[1], (2, N_EDGES), 0, N_NODES, dtype=jnp.int64)
        edge_attr = jax.random.normal(ks[2], (N_EDGES, EDGE_DIM), dtype=jnp.float32)
        conf = jax.random.uniform(ks[3], (N_EDGES, 1), dtype=jnp.float32)
        d_in = IN_CH * 2 + EDGE_DIM
        s1 = 1.0 / np.sqrt(d_in)
        s2 = 1.0 / np.sqrt(OUT_CH)
        s3 = 1.0 / np.sqrt(OUT_CH + 1)
        W1 = jax.random.uniform(ks[4], (d_in, OUT_CH), jnp.float32, -s1, s1)
        b1 = jax.random.uniform(ks[5], (OUT_CH,), jnp.float32, -s1, s1)
        W2 = jax.random.uniform(ks[6], (OUT_CH, OUT_CH), jnp.float32, -s2, s2)
        b2 = jax.random.uniform(ks[7], (OUT_CH,), jnp.float32, -s2, s2)
        Wa = jax.random.uniform(ks[8], (OUT_CH + 1, 1), jnp.float32, -s3, s3)
        ba = jax.random.uniform(ks[9], (1,), jnp.float32, -s3, s3)
        return {'x': x, 'edge_index': edge_index, 'edge_attr': edge_attr, 'calibrated_vlm_conf': conf, 'W1': W1, 'b1': b1, 'W2': W2, 'b2': b2, 'Wa': Wa, 'ba': ba}
    _L0_gnn_all = _L0_gnn_setup()
    _L0_gnn_in = {k: v for k, v in _L0_gnn_all.items() if k in ('W1', 'b1', 'W2', 'b2', 'Wa', 'ba')}
    del _L0_gnn_all
    return {'x': x, 'src': src, 'dst': dst, 'edge_attr_128': edge_attr_128, 'edge_weight1': edge_weight1, 'L0_gnn_W1': _L0_gnn_in['W1'], 'L0_gnn_b1': _L0_gnn_in['b1'], 'L0_gnn_W2': _L0_gnn_in['W2'], 'L0_gnn_b2': _L0_gnn_in['b2'], 'L0_gnn_Wa': _L0_gnn_in['Wa'], 'L0_gnn_ba': _L0_gnn_in['ba']}

def reference(x, src, dst, edge_attr_128, edge_weight1, L0_gnn_W1, L0_gnn_b1, L0_gnn_W2, L0_gnn_b2, L0_gnn_Wa, L0_gnn_ba):
    import jax
    import jax.numpy as jnp

    def _L0_gnn_ref(x, edge_index, edge_attr, calibrated_vlm_conf, W1, b1, W2, b2, Wa, ba):
        import jax, jax.numpy as jnp
        import numpy as np
        N_NODES = 50000
        N_EDGES = 12500
        IN_CH = 128
        OUT_CH = 128
        EDGE_DIM = 128
        row, col = (edge_index[0], edge_index[1])
        src, tgt = (x[row], x[col])
        msg_input = jnp.concatenate([src, tgt, edge_attr], axis=-1)
        h = jax.nn.relu(msg_input @ W1 + b1)
        msg = h @ W2 + b2
        attn_input = jnp.concatenate([msg, calibrated_vlm_conf], axis=-1)
        attn_weight = jax.nn.sigmoid(attn_input @ Wa + ba)
        gated_msg = msg * attn_weight
        out = jax.ops.segment_sum(gated_msg, col, num_segments=x.shape[0])
        return out
    edge_index = jnp.stack([src, dst])
    x = _layernorm(x + _L0_gnn_ref(x, edge_index, edge_attr_128, edge_weight1, L0_gnn_W1, L0_gnn_b1, L0_gnn_W2, L0_gnn_b2, L0_gnn_Wa, L0_gnn_ba), axis=-1)
    return x

_drawn_inputs = setup_inputs


def setup_inputs(seed=0):
    import zlib

    import numpy as np

    out = dict(_drawn_inputs(seed))
    spreads = {}
    factors = {'edge_weight1': 8.0, 'L0_gnn_b1': 8.0, 'L0_gnn_b2': 3.398, 'L0_gnn_Wa': 8.0}
    for name, (base, spread) in spreads.items():
        noise = np.random.default_rng([zlib.crc32(name.encode()), seed]).standard_normal(out[name].shape)
        drawn = base * np.exp(spread * noise) if base else spread * noise
        out[name] = jnp.asarray(drawn.astype(out[name].dtype))
    for name, factor in factors.items():
        out[name] = (out[name] * factor).astype(out[name].dtype)
    return out
```

```python
from contextlib import ExitStack

import concourse.bass as bass
from concourse import mybir
from concourse.alu_op_type import AluOpType as ALU

ACT = mybir.ActivationFunctionType
F32 = mybir.dt.float32
I32 = mybir.dt.int32
AX_X = mybir.AxisListType.X

P = 128
EPS = 1e-5
FAR = 1 << 20
G = 4
SETS = 4
SLOTS = 6
AHEAD = 4
ROWS = 11
STATS = 6


def sizes(n_nodes, n_edges, f):
    tiles = -(-n_edges // P)
    assert tiles % G == 0 and f == P
    groups = tiles // G
    per_part = n_nodes // P
    assert per_part % ROWS == 0
    chunks = per_part // ROWS
    rest = n_nodes - per_part * P
    return tiles, groups, per_part, chunks, rest


def build(nc, x, src, dstw, attr, conf, W1, b1, W2, b2, Wa, ba, out):
    N, F = x.shape
    T, GROUPS, PER, CHUNKS, REST = sizes(N, src.shape[0] * src.shape[1], F)
    PERQ = [(0, 1), (2,), (3, 4), (5,)]
    ITERS = min(GROUPS // SETS, CHUNKS // SLOTS)
    LAST_GROUPS = range(ITERS * SETS, GROUPS)
    LAST_CHUNKS = range(ITERS * SLOTS, CHUNKS)
    ROOT = float(F) ** 0.5
    ACT_ROWS = 6
    ESTEPS = 2 * G
    SSTEPS = 15
    RSQRT_BITS = 0x5F3759DF

    with ExitStack() as ctx:
        def sb(name, shape, dt=F32):
            return ctx.enter_context(nc.sbuf_tensor(name, shape, dt))

        def psum(name, shape):
            return ctx.enter_context(nc.psum_tensor(name, shape, F32))

        def sem(name):
            return ctx.enter_context(nc.semaphore(name))

        def sems(name, n):
            return [sem(f"{name}{i}") for i in range(n)]

        ident = sb("ident", [P, P])
        ones_row = sb("ones_row", [1, P])
        w1 = sb("w1", [P, 3, F])
        b1_col = sb("b1_col", [P, 1])
        w2x = sb("w2x", [P, F + 1])
        w2_turned = sb("w2_turned", [P, P])
        b2x = sb("b2x", [1, F + 1])
        b2_col = sb("b2_col", [P, 1])
        wa_col = sb("wa_col", [P, 1])
        wa_conf = sb("wa_conf", [P, 1])
        ba_one = sb("ba_one", [1, 1])
        src_idx = sb("src_idx", [P, T], I32)
        dst_win = sb("dst_win", [P, T + 2], I32)
        dst_f = sb("dst_f", [P, T + 2])
        gather_idx = sb("gather_idx", [P, GROUPS, 2 * G], I32)
        keep = sb("keep", [P, T])
        is_head = sb("is_head", [P, T])
        skip = sb("skip", [P, T])
        row_idx = sb("row_idx", [P, T], I32)
        logit_lin = sb("logit_lin", [P, T])
        small = sb("small", [P, 16])
        falls = sb("falls", [P, T + 1])
        fall_sum = sb("fall_sum", [P, 1])
        ones_col = sb("ones_col", [P, 1])
        unsorted = sb("unsorted", [1, 1], I32)
        fix_idx = sb("fix_idx", [P, 2], I32)
        idx_slot = sb("idx_slot", [P, SETS, 2 * G], I32)
        rows = sb("rows", [P, SETS, 2 * G, F])
        attr_in = sb("attr_in", [P, SETS, G, F])
        turned = sb("turned", [P, 3, G * P])
        hid = sb("hid", [P, G * P])
        logit = sb("logit", [P, G])
        weight = sb("weight", [P, G])
        gated = sb("gated", [P, SETS, G, F])
        acc = sb("acc", [P, 2, G, F])
        head = sb("head", [P, F])
        e_stats = sb("e_stats", [P, G, STATS])
        e_sc = sb("e_sc", [P, SETS, 8, G])
        stash = sb("stash", [P, T, F])
        ridx_slot = sb("ridx_slot", [P, SETS, G], I32)
        any_dst = sb("any_dst", [P, 1])
        any_later = sb("any_later", [P, 1])
        any_get = sb("any_get", [P, 1], I32)
        any_put = sb("any_put", [P, 1], I32)
        any_zero = sb("any_zero", [P, ROWS * F])
        nodes = sb("nodes", [P, SLOTS, ROWS, F])
        n_stats = sb("n_stats", [P, ROWS, STATS])
        n_sc = sb("n_sc", [P, SLOTS, 8, ROWS])
        rest_in = sb("rest_in", [P, F])
        rest_fix = sb("rest_fix", [P, F])
        match = sb("match", [P, P])
        upper = sb("upper", [P, P])
        r_stats = sb("r_stats", [P, STATS])
        r_sc = sb("r_sc", [P, 8, 1])

        messages = nc.dram_tensor("messages", (P, T, F), F32, kind="Internal").ap()
        sums_by_node = nc.dram_tensor("sums_by_node", (N, F), F32, kind="Internal").ap()

        turn_ps = psum("turn_ps", [P, 3, G * P])
        hid_ps = psum("hid_ps", [P, G * P])
        msg_ps = psum("msg_ps", [P, 2, 512])
        misc_ps = psum("misc_ps", [P, 512])

        def msg(j):
            return msg_ps[:, j // 2, (j % 2) * 256:(j % 2) * 256 + F + 1]

        consts_in = sem("consts_in")
        edges_in = sem("edges_in")
        pool_const = sem("pool_const")
        w2_in_ps = sem("w2_in_ps")
        w2_turned_ok = sem("w2_turned_ok")
        wa_in_ps = sem("wa_in_ps")
        w2_ready = sem("w2_ready")
        lin_ready = sem("lin_ready")
        prep = sem("prep")
        idx_ready = sems("idx_ready", SETS)
        gathered = sems("gathered", SETS)
        attr_landed = sems("attr_landed", SETS)
        turned_ps_ready = sem("turned_ps_ready")
        turned_ready = sem("turned_ready")
        hid_ps_ready = sem("hid_ps_ready")
        hid_ready = sem("hid_ready")
        msg_ready = sem("msg_ready")
        logit_ready = sem("logit_ready")
        weight_ready = sem("weight_ready")
        gated_ready = sem("gated_ready")
        edge_step = sem("edge_step")
        rows_free = sems("rows_free", SETS)
        x_landed = sems("x_landed", SLOTS)
        node_stat = sem("node_stat")
        node_step = sem("node_step")
        scale_ready = sems("scale_ready", SLOTS)
        act_normed = sems("act_normed", SLOTS)
        dve_normed = sems("dve_normed", SLOTS)
        stored = sems("stored", SLOTS)
        rest_landed = sem("rest_landed")
        rest_normed = sem("rest_normed")
        rest_stored = sem("rest_stored")
        e_stat = sem("e_stat")
        e_scale = sems("e_scale", SETS)
        final_step = sem("final_step")
        rest_step = sem("rest_step")
        rest_scale = sem("rest_scale")
        fix_step = sem("fix_step")
        ridx_ready = sems("ridx_ready", SETS)
        out_ready = sems("out_ready", SETS)
        scattered = sems("scattered", SETS)
        fix_idx_ready = sem("fix_idx_ready")
        fix_gathered = sem("fix_gathered")
        first_ps = sem("first_ps")
        match_ready = sem("match_ready")
        tails_ps = sem("tails_ps")
        fix_ready = sem("fix_ready")
        fix_scattered = sem("fix_scattered")

        saved = sems("saved", SETS)
        fall_ready = sem("fall_ready")
        fall_ps = sem("fall_ps")
        flag_ready = sem("flag_ready")
        any_start = sem("any_start")
        any_zeroed = sem("any_zeroed")
        any_cleared = sem("any_cleared")
        any_loaded = sem("any_loaded")
        any_dst_ready = sem("any_dst_ready")
        any_dst_ps = sem("any_dst_ps")
        any_same_step = sem("any_same_step")
        any_same_ready = sem("any_same_ready")
        any_sum_ps = sem("any_sum_ps")
        any_got = sem("any_got")
        any_new = sem("any_new")
        any_put_done = sem("any_put_done")
        all_idx_ready = sem("all_idx_ready")
        all_got = sem("all_got")
        all_step = sem("all_step")
        all_scale = sem("all_scale")
        all_ready = sem("all_ready")
        all_written = sem("all_written")

        block = ctx.enter_context(nc.Block())

        def wait(eng, semaphore, value):
            if not (isinstance(value, int) and value <= 0):
                eng.wait_ge(semaphore, value)

        attr_rows = attr.rearrange("(p t) f -> p t f", p=P)
        x_main = x[0:PER * P].rearrange("(p r) f -> p r f", p=P)
        out_main = out[0:PER * P].rearrange("(p r) f -> p r f", p=P)

        def chunk_of(view, c):
            return view[:, bass.ds(c * ROWS, ROWS), :]

        def tiles_of(t, g, n=G):
            return t[:, bass.ds(g * G, n)]

        @block.sync
        def _(sp):
            for dst, source in ((src_idx[:], src), (dst_win[:], dstw), (logit_lin[:], conf)):
                sp.dma_start(dst, source).then_inc(edges_in, 16)
            consts = [
                (w1[:], W1.rearrange("(c k) o -> k c o", c=3)),
                (b1_col[:], b1.rearrange("(o u) -> o u", u=1)),
                (w2x[:, 0:F], W2),
                (b2x[0:1, 0:F], b2.rearrange("(u o) -> u o", u=1)),
                (b2_col[:], b2.rearrange("(o u) -> o u", u=1)),
                (wa_col[:], Wa[0:F, :]),
                (wa_conf[:], Wa[F:F + 1, :].partition_broadcast(P)),
                (ba_one[:], ba.rearrange("(u o) -> u o", u=1)),
            ]
            for dst, source in consts:
                sp.dma_start(dst, source).then_inc(consts_in, 16)

            def load_nodes(c, u):
                sp.dma_start(nodes[:, u], chunk_of(x_main, c)).then_inc(x_landed[u], 16)

            def load_attr(g, s):
                sp.dma_start(attr_in[:, s], tiles_of(attr_rows, g)).then_inc(attr_landed[s], 16)

            def store_nodes(c, u, it):
                sp.wait_ge(act_normed[u], it + 1)
                sp.wait_ge(dve_normed[u], it + 1)
                sp.dma_start(chunk_of(out_main, c), nodes[:, u]).then_inc(stored[u], 16)

            def save_messages(g, nth, s):
                sp.wait_ge(gated_ready, G * (g + 1))
                sp.dma_start(tiles_of(messages, g), gated[:, s]).then_inc(saved[s], 16)

            def quarter(it, s, us):
                sp.wait_ge(turned_ps_ready, 3 * (it * SETS + s + 1))
                load_attr(it * SETS + s + SETS, s)
                for u in us:
                    u2 = (u + AHEAD) % SLOTS
                    wait(sp, stored[u2], 16 * (it + 1) if u + AHEAD >= SLOTS else 16 * it)
                    load_nodes(it * SLOTS + u + AHEAD, u2)
                    store_nodes(it * SLOTS + u, u, it)
                save_messages(it * SETS + s, it + 1, s)

            for c in range(AHEAD):
                load_attr(c, c)
                load_nodes(c, c)
            sp.dma_start(rest_in[0:REST, :], x[PER * P:N, :]).then_inc(rest_landed, 16)
            for s in range(SETS):
                quarter(0, s, PERQ[s])
            with sp.Fori(1, ITERS) as it:
                for s in range(SETS):
                    quarter(it, s, PERQ[s])
            for g in LAST_GROUPS:
                it, s = g // SETS, g % SETS
                if g + SETS < GROUPS:
                    sp.wait_ge(turned_ps_ready, 3 * (g + 1))
                    load_attr(g + SETS, s)
                cs = [LAST_CHUNKS[g - LAST_GROUPS[0]]] if g - LAST_GROUPS[0] < len(LAST_CHUNKS) else []
                for c in cs:
                    if c + AHEAD < CHUNKS:
                        u2 = (c + AHEAD) % SLOTS
                        sp.wait_ge(stored[u2], 16 * ((c + AHEAD) // SLOTS))
                        load_nodes(c + AHEAD, u2)
                    store_nodes(c, c % SLOTS, c // SLOTS)
                save_messages(g, it + 1, s)
            sp.wait_ge(rest_normed, 1)
            sp.dma_start(out[PER * P:N, :], rest_in[0:REST, :]).then_inc(rest_stored, 16)

            def sort_out(sp):
                sp.wait_ge(any_start, 1)
                sp.wait_ge(any_zeroed, 1)
                zeros = any_zero[:].rearrange("p (r f) -> p r f", f=F)
                sums_main = sums_by_node[0:PER * P].rearrange("(p r) f -> p r f", p=P)
                with sp.Fori(0, CHUNKS) as c:
                    sp.dma_start(chunk_of(sums_main, c), zeros).then_inc(any_cleared, 16)
                sp.dma_start(sums_by_node[PER * P:N, :], any_zero[0:REST, 0:F]).then_inc(any_cleared, 16)
                with sp.Fori(1, T + 1) as nth:
                    sp.wait_ge(any_start, nth)
                    sp.dma_start(gated[:, 0, 0, :], messages[:, bass.ds(nth - 1, 1), :].rearrange("p u f -> p (u f)")
                                 ).then_inc(any_loaded, 16)

            sp.wait_ge(flag_ready, 1)
            with sp.If(sp.value_load(unsorted[0:1, 0:1], min_val=0, max_val=1) > 0):
                sort_out(sp)
            sp.nop()

        @block.gpsimd
        def _(pool):
            pool.memset(ident[:], 0.0).then_inc(pool_const, 1)
            pool.memset(ones_row[:], 1.0).then_inc(pool_const, 1)
            pool.memset(head[:], 0.0).then_inc(pool_const, 1)
            pool.memset(acc[:], 0.0).then_inc(pool_const, 1)
            pool.memset(upper[:], 1.0).then_inc(pool_const, 1)
            pool.memset(ones_col[:], 1.0).then_inc(pool_const, 1)
            pool.wait_ge(pool_const, 6)
            pool.affine_select(out=upper[:], in_=upper[:], compare_op=ALU.is_gt, fill=0.0, base=0,
                               pattern=[[1, P]], channel_multiplier=-1).then_inc(pool_const, 1)
            pool.affine_select(out=ident[:], in_=ident[:], compare_op=ALU.not_equal, fill=1.0, base=0,
                               pattern=[[-1, P]], channel_multiplier=1).then_inc(pool_const, 1)

            def gather(nth, s):
                pool.wait_ge(pool_const, 8)
                pool.wait_ge(idx_ready[s], nth)
                pool.wait_ge(rows_free[s], nth)
                for j in range(2 * G):
                    pool.indirect_dma_start(
                        out=rows[:, s, j, :], out_offset=None, in_=x[:, :],
                        in_offset=bass.IndirectOffsetOnAxis(ap=idx_slot[:, s, j:j + 1], axis=0),
                    ).then_inc(gathered[s], 16)

            for s in range(SETS):
                pool.sem_inc(rows_free[s], 1)
            with pool.Fori(1, ITERS + 1) as nth:
                for s in range(SETS):
                    gather(nth, s)
            for g in LAST_GROUPS:
                gather(g // SETS + 1, g % SETS)
            pool.wait_ge(fix_idx_ready, 1)
            pool.indirect_dma_start(
                out=rest_fix[:, :], out_offset=None, in_=x[:, :],
                in_offset=bass.IndirectOffsetOnAxis(ap=fix_idx[:, 0:1], axis=0),
            ).then_inc(fix_gathered, 16)

            for u in range(SLOTS):
                pool.wait_ge(stored[u], 16 * len(range(u, CHUNKS, SLOTS)))
            pool.wait_ge(rest_stored, 16)

            def scatter(nth, s):
                pool.wait_ge(pool_const, 8)
                pool.wait_ge(out_ready[s], nth)
                pool.wait_ge(ridx_ready[s], nth)
                for j in range(G):
                    pool.indirect_dma_start(
                        out=out[:, :], out_offset=bass.IndirectOffsetOnAxis(ap=ridx_slot[:, s, j:j + 1], axis=0),
                        in_=gated[:, s, j, :], in_offset=None, bounds_check=N - 1, oob_is_err=False,
                    ).then_inc(scattered[s], 16)

            with pool.Fori(1, GROUPS // SETS + 1) as nth:
                for s in range(SETS):
                    scatter(nth, s)
            for g in range(GROUPS // SETS * SETS, GROUPS):
                scatter(g // SETS + 1, g % SETS)
            pool.wait_ge(fix_ready, 1)
            pool.indirect_dma_start(
                out=out[:, :], out_offset=bass.IndirectOffsetOnAxis(ap=fix_idx[:, 1:2], axis=0),
                in_=rest_in[:, :], in_offset=None, bounds_check=N - 1, oob_is_err=False,
            ).then_inc(fix_scattered, 16)
            for s in range(SETS):
                pool.wait_ge(scattered[s], 16 * G * len(range(s, GROUPS, SETS)))
            pool.wait_ge(fix_scattered, 16)

            def get(to, table, idx, semaphore):
                pool.indirect_dma_start(
                    out=to, out_offset=None, in_=table[:, :],
                    in_offset=bass.IndirectOffsetOnAxis(ap=idx, axis=0)).then_inc(semaphore, 16)

            def put(table, idx, rows_, semaphore):
                pool.indirect_dma_start(
                    out=table[:, :], out_offset=bass.IndirectOffsetOnAxis(ap=idx, axis=0),
                    in_=rows_, in_offset=None, bounds_check=N - 1, oob_is_err=False).then_inc(semaphore, 16)

            def sort_out():
                for s in range(SETS):
                    pool.wait_ge(saved[s], 16 * len(range(s, GROUPS, SETS)))
                pool.sem_inc(any_start, 1)
                pool.wait_ge(any_cleared, 16 * (CHUNKS + 1))
                with pool.Fori(1, T + 1) as nth:
                    pool.wait_ge(pool_const, 8)
                    pool.wait_ge(any_same_ready, nth)
                    get(rows[:, 0, 0, :], sums_by_node, any_get[:, 0:1], any_got)
                    pool.wait_ge(pool_const, 8)
                    pool.wait_ge(any_new, nth)
                    put(sums_by_node, any_put[:, 0:1], rows[:, 0, 1, :], any_put_done)
                    pool.wait_ge(any_put_done, nth * 16)
                    pool.sem_inc(any_start, 1)
                with pool.Fori(1, T + 1) as nth:
                    pool.wait_ge(pool_const, 8)
                    pool.wait_ge(all_idx_ready, nth)
                    get(rows[:, 0, 0, :], sums_by_node, any_get[:, 0:1], all_got)
                    get(rows[:, 0, 1, :], x, any_get[:, 0:1], all_got)
                    pool.wait_ge(pool_const, 8)
                    pool.wait_ge(all_ready, nth)
                    put(out, any_put[:, 0:1], rows[:, 0, 3, :], all_written)
                pool.wait_ge(all_written, 16 * T)

            pool.wait_ge(flag_ready, 1)
            with pool.If(pool.value_load(unsorted[0:1, 0:1], min_val=0, max_val=1) > 0):
                sort_out()
            pool.nop()

        @block.scalar
        def _(act):
            def edges(g, g_it, s):
                for c in range(3):
                    act.wait_ge(turned_ps_ready, g * 3 + c + 1)
                    if c == 0:
                        wait(act, hid_ps_ready, g)
                    act.activation(turned[:, c], turn_ps[:, c], ACT.Copy).then_inc(turned_ready, 1)
                act.wait_ge(hid_ps_ready, g + 1)
                wait(act, msg_ready, g)
                act.wait_ge(consts_in, 16 * 8)
                act.activation(hid[:], hid_ps[:], ACT.Relu, bias=b1_col[:, 0:1]).then_inc(hid_ready, 1)

            def gates(g, g_it, s):
                act.wait_ge(logit_ready, g + 1)
                wait(act, gated_ready, G * g)
                act.activation(weight[:], logit[:], ACT.Sigmoid).then_inc(weight_ready, 1)
                act.wait_ge(weight_ready, g + 1)
                wait(act, rows_free[s], g_it + 1)
                wait(act, saved[s], 16 * g_it)
                for j in range(G):
                    act.activation(gated[:, s, j, :], msg(j)[:, 0:F], ACT.Copy,
                                   scale=weight[:, j:j + 1]).then_inc(gated_ready, 1)

            def norm(u, it):
                act.wait_ge(scale_ready[u], 2 * (it + 1))
                for r in range(ACT_ROWS):
                    last = act.activation(nodes[:, u, r, :], nodes[:, u, r, :], ACT.Identity,
                                          scale=n_sc[:, u, 6, r:r + 1], bias=n_sc[:, u, 7, r:r + 1])
                last.then_inc(act_normed[u], 1)

            def quarter(g, g_it, s, c_it, us):
                edges(g, g_it, s)
                for u in us[:1]:
                    norm(u, c_it)
                gates(g, g_it, s)
                for u in us[1:]:
                    norm(u, c_it)

            for s in range(SETS):
                quarter(s, 0, s, 0, PERQ[s])
            with act.Fori(1, ITERS) as it:
                for s in range(SETS):
                    quarter(it * SETS + s, it, s, it, PERQ[s])
            for i, g in enumerate(LAST_GROUPS):
                cs = [LAST_CHUNKS[i]] if i < len(LAST_CHUNKS) else []
                quarter(g, g // SETS, g % SETS, cs[0] // SLOTS if cs else 0, [c % SLOTS for c in cs])

            def fetch(g, g_it, s):
                wait(act, scattered[s], 16 * G * g_it)
                act.wait_ge(e_scale[s], 2 * (g_it + 1))
                for j in range(G):
                    last = act.activation(gated[:, s, j, :], stash[:, bass.ds(g * G + j, 1), :].rearrange("p u f -> p (u f)"),
                                          ACT.Identity, scale=e_sc[:, s, 6, j:j + 1], bias=e_sc[:, s, 7, j:j + 1])
                last.then_inc(out_ready[s], 1)

            for s in range(SETS):
                act.wait_ge(saved[s], 16 * len(range(s, GROUPS, SETS)))
            for s in range(SETS):
                fetch(s, 0, s)
            with act.Fori(1, GROUPS // SETS) as it:
                for s in range(SETS):
                    fetch(it * SETS + s, it, s)
            for g in range(GROUPS // SETS * SETS, GROUPS):
                fetch(g, g // SETS, g % SETS)

        @block.tensor
        def _(pe):
            pe.wait_ge(pool_const, 8)
            pe.wait_ge(consts_in, 16 * 8)
            pe.transpose(misc_ps[:, 0:P], w2x[:, 0:F], ident[:]).then_inc(w2_in_ps, 1)
            pe.wait_ge(w2_turned_ok, 1)
            pe.matmul(misc_ps[:, 256:257], w2_turned[:], wa_col[:], start=True, stop=True)
            pe.matmul(misc_ps[0:1, 260:261], b2_col[:], wa_col[:], start=True, stop=True).then_inc(wa_in_ps, 1)

            def group(g, g_it, s):
                pe.wait_ge(gathered[s], 16 * 2 * G * (g_it + 1))
                for c in range(3):
                    if c == 2:
                        pe.wait_ge(attr_landed[s], 16 * (g_it + 1))
                    if c == 0:
                        wait(pe, turned_ready, 3 * g)
                    for j in range(G):
                        tile = attr_in[:, s, j, :] if c == 2 else rows[:, s, c * G + j, :]
                        last = pe.transpose(turn_ps[:, c, j * P:(j + 1) * P], tile, ident[:])
                    last.then_inc(turned_ps_ready, 1)
                wait(pe, hid_ready, g)
                pe.wait_ge(turned_ready, 3 * g + 3)
                for c in range(3):
                    last = pe.matmul(hid_ps[:], w1[:, c, :], turned[:, c, :], start=(c == 0), stop=(c == 2))
                last.then_inc(hid_ps_ready, 1)
                pe.wait_ge(hid_ready, g + 1)
                wait(pe, gated_ready, G * g)
                pe.wait_ge(w2_ready, 2)
                for j in range(G):
                    pe.matmul(msg(j), hid[:, j * P:(j + 1) * P], w2x[:], start=True, stop=False)
                    last = pe.matmul(msg(j), ones_row[:], b2x[:], start=False, stop=True)
                last.then_inc(msg_ready, 1)

            for s in range(SETS):
                group(s, 0, s)
            with pe.Fori(1, ITERS) as it:
                for s in range(SETS):
                    group(it * SETS + s, it, s)
            for g in LAST_GROUPS:
                group(g, g // SETS, g % SETS)

            pe.wait_ge(prep, 1)
            pe.matmul(misc_ps[:, 0:P], dst_f[:, 1:2].to_broadcast([P, P]), ident[:], start=True,
                      stop=True).then_inc(first_ps, 1)
            pe.wait_ge(match_ready, 1)
            lg = LAST_GROUPS[-1]
            pe.wait_ge(edge_step, ESTEPS * (lg + 1))
            pe.matmul(misc_ps[:, 0:P], match[:], acc[:, lg % 2, G - 1, :], start=True,
                      stop=True).then_inc(tails_ps, 1)
            pe.wait_ge(fall_ready, 1)
            pe.wait_ge(hid_ready, GROUPS)
            pe.matmul(hid_ps[0:1, 300:301], fall_sum[:], ones_col[:], start=True, stop=True).then_inc(fall_ps, 1)

            def sort_out():
                pe.wait_ge(fix_ready, 1)
                with pe.Fori(1, T + 1) as nth:
                    pe.wait_ge(any_dst_ready, nth)
                    pe.matmul(misc_ps[:, 0:P], any_dst[:, 0:1].to_broadcast([P, P]), ident[:], start=True,
                              stop=True).then_inc(any_dst_ps, 1)
                    pe.wait_ge(any_same_ready, nth)
                    pe.wait_ge(any_loaded, nth * 16)
                    pe.matmul(hid_ps[:, 0:P], match[:], gated[:, 0, 0, :], start=True,
                              stop=True).then_inc(any_sum_ps, 1)

            pe.wait_ge(flag_ready, 1)
            with pe.If(pe.value_load(unsorted[0:1, 0:1], min_val=0, max_val=1) > 0):
                sort_out()
            pe.nop()

        @block.vector
        def _(dve):
            done = [0]

            def step(ins):
                done[0] += 1
                ins.then_inc(prep, 1)

            def settle():
                dve.wait_ge(prep, done[0])

            dve.wait_ge(edges_in, 16 * 3)
            d, before, after = dst_f[:, 1:T + 1], dst_f[:, 0:T], dst_f[:, 2:T + 2]
            step(dve.tensor_copy(dst_f[:], dst_win[:]))
            step(dve.tensor_copy(gather_idx[:, :, 0:G], src_idx[:].rearrange("p (g j) -> p g j", j=G)))
            settle()
            step(dve.tensor_scalar(gather_idx[:, :, G:2 * G], dst_f[:, 1:T + 1].rearrange("p (g j) -> p g j", j=G),
                                   float(N - 1), None, ALU.min))
            settle()
            for s in range(SETS):
                dve.tensor_copy(idx_slot[:, s], gather_idx[:, s]).then_inc(idx_ready[s], 1)
            step(dve.tensor_tensor(keep[:], d, before, ALU.is_equal))
            step(dve.tensor_scalar(is_head[:], d, dst_f[:, 0:1], None, ALU.is_equal))
            step(dve.tensor_tensor(skip[:], d, after, ALU.is_equal))
            step(dve.tensor_tensor(falls[:], dst_f[:, 0:T + 1], dst_f[:, 1:T + 2], ALU.is_gt))
            settle()
            step(dve.memset(keep[:, 0:1], 0.0))
            dve.tensor_reduce(fall_sum[:], falls[:], AX_X, ALU.add).then_inc(fall_ready, 1)
            step(dve.tensor_tensor(skip[:], skip[:], is_head[:], ALU.add))
            settle()
            step(dve.scalar_tensor_tensor(row_idx[:], skip[:], float(FAR), d, ALU.mult, ALU.add))
            first, last_, prev, nxt = dst_f[:, 1:2], dst_f[:, T:T + 1], dst_f[:, 0:1], dst_f[:, T + 1:T + 2]
            step(dve.tensor_tensor(small[:, 0:1], first, prev, ALU.is_equal))
            step(dve.tensor_tensor(small[:, 1:2], first, last_, ALU.is_equal))
            step(dve.tensor_tensor(small[:, 2:3], nxt, last_, ALU.is_equal))
            settle()
            step(dve.tensor_tensor(small[:, 3:4], small[:, 1:2], small[:, 2:3], ALU.mult))
            settle()
            step(dve.tensor_scalar(small[:, 4:5], small[:, 3:4], -1.0, 1.0, ALU.mult, ALU.add))
            settle()
            step(dve.tensor_tensor(small[:, 5:6], small[:, 4:5], small[:, 0:1], ALU.mult))
            settle()
            step(dve.tensor_scalar(small[:, 6:7], small[:, 5:6], -float(FAR), float(FAR), ALU.mult, ALU.add))
            settle()
            step(dve.tensor_tensor(fix_idx[:, 1:2], small[:, 6:7], first, ALU.add))
            settle()
            dve.tensor_copy(fix_idx[:, 0:1], first).then_inc(fix_idx_ready, 1)
            dve.wait_ge(consts_in, 16 * 8)
            step(dve.tensor_scalar(logit_lin[:], logit_lin[:], wa_conf[:, 0:1], None, ALU.mult))
            dve.wait_ge(w2_in_ps, 1)
            dve.tensor_copy(w2_turned[:], misc_ps[:, 0:P]).then_inc(w2_turned_ok, 1)
            dve.wait_ge(wa_in_ps, 1)
            dve.tensor_copy(w2x[:, F:F + 1], misc_ps[:, 256:257]).then_inc(w2_ready, 1)
            dve.tensor_tensor(b2x[0:1, F:F + 1], misc_ps[0:1, 260:261], ba_one[:], ALU.add).then_inc(w2_ready, 1)
            settle()
            dve.wait_ge(pool_const, 8)

            def scales(st, sc, sem_, base, final):
                mean_e, m2_e, mean_o, m2_o = (st[:, :, k] for k in (1, 2, 4, 5))
                mean2, apart, v, y, a = (sc[:, k] for k in range(5))
                n = [0]

                def then(ins, wait=True):
                    n[0] += 1
                    ins.then_inc(sem_, 1)
                    if wait:
                        dve.wait_ge(sem_, base + n[0])

                then(dve.tensor_tensor(mean2, mean_e, mean_o, ALU.add), False)
                then(dve.tensor_tensor(apart, mean_e, mean_o, ALU.subtract), False)
                then(dve.tensor_tensor(v, m2_e, m2_o, ALU.add))
                then(dve.scalar_tensor_tensor(a, apart, F / 4.0, apart, ALU.mult, ALU.mult))
                then(dve.scalar_tensor_tensor(v, v, F * EPS, a, ALU.add, ALU.add))
                then(dve.tensor_scalar(y.bitcast(I32), v.bitcast(I32), -0.5, float(RSQRT_BITS), ALU.mult, ALU.add))
                for three in (3.0, 12.0, 768.0):
                    then(dve.tensor_tensor(a, y, y, ALU.mult))
                    then(dve.tensor_tensor(a, a, v, ALU.mult))
                    then(dve.scalar_tensor_tensor(y, a, -three, y, ALU.add, ALU.mult))
                dve.tensor_scalar(sc[:, 6], y, -ROOT / 8192, None, ALU.mult).then_inc(final, 1)
                dve.scalar_tensor_tensor(sc[:, 7], mean2, 0.5 * ROOT / 8192, y, ALU.mult, ALU.mult).then_inc(final, 1)
                assert n[0] == SSTEPS

            def node_stats(c, u, it):
                dve.wait_ge(x_landed[u], 16 * (it + 1))
                for r in range(ROWS):
                    last = dve.bn_stats(n_stats[:, r, :], nodes[:, u, r, :])
                last.then_inc(node_stat, 1)
                dve.wait_ge(node_stat, c + 1)
                scales(n_stats[:], n_sc[:, u], node_step, SSTEPS * c, scale_ready[u])

            def node_norm(u, it):
                dve.wait_ge(scale_ready[u], 2 * (it + 1))
                for r in range(ACT_ROWS, ROWS):
                    last = dve.tensor_scalar(nodes[:, u, r, :], nodes[:, u, r, :], n_sc[:, u, 6, r:r + 1],
                                             n_sc[:, u, 7, r:r + 1], ALU.mult, ALU.add)
                last.then_inc(dve_normed[u], 1)

            def turn(g, g_it, s, more_idx):
                dve.wait_ge(gathered[s], 16 * 2 * G * (g_it + 1))
                if more_idx:
                    dve.tensor_copy(idx_slot[:, s], gather_idx[:, bass.ds(g + SETS, 1), :].rearrange("p u j -> p (u j)")
                                    ).then_inc(idx_ready[s], 1)

            def logits(g):
                dve.wait_ge(msg_ready, g + 1)
                wait(dve, weight_ready, g)
                dve.tensor_tensor(logit[:].rearrange("p (a b) -> p a b", a=2), msg_ps[:, :, F:512:256],
                                  tiles_of(logit_lin, g).rearrange("p (a b) -> p a b", a=2),
                                  ALU.add).then_inc(logit_ready, 1)

            def sums(g, g_it, s):
                base = ESTEPS * g
                wait(dve, edge_step, base)
                b = s % 2
                dve.wait_ge(gated_ready, G * g + G)
                for j in range(G):
                    prev_acc = acc[:, b, j - 1, :] if j else acc[:, 1 - b, G - 1, :]
                    if j:
                        dve.wait_ge(edge_step, base + 2 * j)
                    dve.scalar_tensor_tensor(acc[:, b, j, :], prev_acc, keep[:, bass.ds(g * G + j, 1)],
                                             gated[:, s, j, :], ALU.mult, ALU.add).then_inc(edge_step, 1)
                    dve.scalar_tensor_tensor(head[:], gated[:, s, j, :], is_head[:, bass.ds(g * G + j, 1)],
                                             head[:], ALU.mult, ALU.add).then_inc(edge_step, 1)
                dve.wait_ge(edge_step, base + 2 * G)
                dve.tensor_tensor(tiles_of(stash, g), acc[:, b], rows[:, s, G:2 * G, :], ALU.add
                                  ).then_inc(rows_free[s], 1)

            def quarter(g, g_it, s, c0, c_it, us, more_idx):
                turn(g, g_it, s, more_idx)
                for u in us:
                    node_stats(c0 + u, u, c_it)
                logits(g)
                for u in us:
                    node_norm(u, c_it)
                sums(g, g_it, s)

            for s in range(SETS):
                quarter(s, 0, s, 0, 0, PERQ[s], True)
            with dve.Fori(1, ITERS) as it:
                for s in range(SETS):
                    quarter(it * SETS + s, it, s, it * SLOTS, it, PERQ[s], True)
            for i, g in enumerate(LAST_GROUPS):
                cs = [LAST_CHUNKS[i]] if i < len(LAST_CHUNKS) else []
                c_it = cs[0] // SLOTS if cs else 0
                quarter(g, g // SETS, g % SETS, c_it * SLOTS, c_it, [c % SLOTS for c in cs], g + SETS < GROUPS)

            dve.wait_ge(rest_landed, 16)
            dve.bn_stats(r_stats[0:REST, :], rest_in[0:REST, :]).then_inc(rest_step, 1)
            dve.wait_ge(rest_step, 1)
            scales(r_stats[0:REST].rearrange("p (u k) -> p u k", u=1), r_sc[0:REST], rest_step, 1, rest_scale)
            dve.wait_ge(rest_scale, 2)
            dve.tensor_scalar(rest_in[0:REST, :], rest_in[0:REST, :], r_sc[0:REST, 6, :], r_sc[0:REST, 7, :],
                              ALU.mult, ALU.add).then_inc(rest_normed, 1)

            def finish(g, g_it, s):
                wait(dve, scattered[s], 16 * G * g_it)
                dve.tensor_copy(ridx_slot[:, s], tiles_of(row_idx, g)).then_inc(ridx_ready[s], 1)
                for j in range(G):
                    last = dve.bn_stats(e_stats[:, j, :], stash[:, bass.ds(g * G + j, 1), :].rearrange("p u f -> p (u f)"))
                last.then_inc(e_stat, 1)
                dve.wait_ge(e_stat, g + 1)
                wait(dve, out_ready[s], g_it)
                scales(e_stats[:], e_sc[:, s], final_step, SSTEPS * g, e_scale[s])

            for s in range(SETS):
                dve.wait_ge(rows_free[s], 1 + len(range(s, GROUPS, SETS)))
            for s in range(SETS):
                finish(s, 0, s)

            dve.wait_ge(first_ps, 1)
            dve.tensor_scalar(match[:], misc_ps[:, 0:P], last_, None, ALU.is_equal).then_inc(fix_step, 1)
            dve.wait_ge(fix_step, 1)
            dve.tensor_tensor(match[:], match[:], upper[:], ALU.mult).then_inc(match_ready, 1)
            dve.wait_ge(fix_gathered, 16)
            dve.tensor_tensor(rest_fix[:], rest_fix[:], head[:], ALU.add).then_inc(fix_step, 1)
            dve.wait_ge(fix_step, 2)
            dve.wait_ge(tails_ps, 1)
            dve.tensor_tensor(rest_fix[:], rest_fix[:], misc_ps[:, 0:P], ALU.add).then_inc(fix_step, 1)
            dve.wait_ge(fix_step, 3)
            dve.wait_ge(rest_normed, 1)
            dve.bn_stats(r_stats[:, :], rest_fix[:, :]).then_inc(rest_step, 1)
            dve.wait_ge(rest_step, SSTEPS + 2)
            scales(r_stats[:].rearrange("p (u k) -> p u k", u=1), r_sc[:], rest_step, SSTEPS + 2, rest_scale)
            dve.wait_ge(rest_scale, 4)
            dve.wait_ge(rest_stored, 16)
            dve.tensor_scalar(rest_in[:], rest_fix[:], r_sc[:, 6, :], r_sc[:, 7, :],
                              ALU.mult, ALU.add).then_inc(fix_ready, 1)

            with dve.Fori(1, GROUPS // SETS) as it:
                for s in range(SETS):
                    finish(it * SETS + s, it, s)
            for g in range(GROUPS // SETS * SETS, GROUPS):
                finish(g, g // SETS, g % SETS)

            dve.wait_ge(fall_ps, 1)
            dve.tensor_scalar(unsorted[:], hid_ps[0:1, 300:301], 1.0, None, ALU.min).then_inc(flag_ready, 1)

            def sort_out():
                dve.wait_ge(any_start, 1)
                dve.memset(any_zero[:], 0.0).then_inc(any_zeroed, 1)
                with dve.Fori(1, T + 1) as nth:
                    dve.wait_ge(any_start, nth)
                    dst_of = dst_f[:, bass.ds(nth, 1)]
                    dve.tensor_copy(any_dst[:], dst_of).then_inc(any_dst_ready, 1)
                    dve.tensor_scalar(any_get[:], dst_of, float(N - 1), None, ALU.min).then_inc(any_same_step, 1)
                    dve.wait_ge(any_dst_ready, nth)
                    dve.wait_ge(any_dst_ps, nth)
                    dve.tensor_scalar(match[:], misc_ps[:, 0:P], any_dst[:, 0:1], None, ALU.is_equal
                                      ).then_inc(any_same_step, 1)
                    dve.wait_ge(any_same_step, nth * 5 - 3)
                    dve.tensor_tensor(rest_in[:], match[:], upper[:], ALU.mult).then_inc(any_same_step, 1)
                    dve.wait_ge(any_same_step, nth * 5 - 2)
                    dve.tensor_reduce(any_later[:], rest_in[:], AX_X, ALU.add).then_inc(any_same_step, 1)
                    dve.wait_ge(any_same_step, nth * 5 - 1)
                    dve.scalar_tensor_tensor(any_put[:], any_later[:], float(FAR), any_dst[:], ALU.mult, ALU.add
                                             ).then_inc(any_same_step, 1)
                    dve.wait_ge(any_same_step, nth * 5)
                    dve.tensor_copy(row_idx[:, bass.ds(nth - 1, 1)], any_put[:]).then_inc(any_same_ready, 1)
                    dve.wait_ge(any_got, nth * 16)
                    dve.wait_ge(any_sum_ps, nth)
                    dve.tensor_tensor(rows[:, 0, 1, :], rows[:, 0, 0, :], hid_ps[:, 0:P], ALU.add).then_inc(any_new, 1)
                dve.wait_ge(any_start, T + 1)
                with dve.Fori(1, T + 1) as nth:
                    dve.tensor_scalar(any_get[:], dst_f[:, bass.ds(nth, 1)], float(N - 1), None, ALU.min
                                      ).then_inc(all_step, 1)
                    dve.wait_ge(all_step, nth * (SSTEPS + 3) - (SSTEPS + 2))
                    dve.tensor_copy(any_put[:], row_idx[:, bass.ds(nth - 1, 1)]).then_inc(all_idx_ready, 1)
                    dve.wait_ge(all_got, nth * 32)
                    dve.tensor_tensor(rows[:, 0, 2, :], rows[:, 0, 0, :], rows[:, 0, 1, :], ALU.add).then_inc(all_step, 1)
                    dve.wait_ge(all_step, nth * (SSTEPS + 3) - (SSTEPS + 1))
                    dve.bn_stats(r_stats[:], rows[:, 0, 2, :]).then_inc(all_step, 1)
                    dve.wait_ge(all_step, nth * (SSTEPS + 3) - SSTEPS)
                    scales(r_stats[:].rearrange("p (u k) -> p u k", u=1), r_sc[:], all_step,
                           nth * (SSTEPS + 3) - SSTEPS, all_scale)
                    dve.wait_ge(all_scale, nth * 2)
                    dve.tensor_scalar(rows[:, 0, 3, :], rows[:, 0, 2, :], r_sc[:, 6, :], r_sc[:, 7, :],
                                      ALU.mult, ALU.add).then_inc(all_ready, 1)
                    dve.wait_ge(all_written, nth * 16)

            dve.wait_ge(flag_ready, 1)
            with dve.If(dve.value_load(unsorted[0:1, 0:1], min_val=0, max_val=1) > 0):
                sort_out()
            dve.engine_nop()


def kernel(x, src, dst, edge_attr_128, edge_weight1, L0_gnn_W1, L0_gnn_b1, L0_gnn_W2, L0_gnn_b2, L0_gnn_Wa,
           L0_gnn_ba):
    import numpy as np
    import concourse.bacc as bacc
    from concourse.bass_utils import run_bass_kernel_spmd

    N, F = x.shape
    E = src.shape[0]
    T = -(-E // (P * G)) * G
    fill = P * T - E
    dst = np.ascontiguousarray(dst)
    line = np.concatenate([np.full(1, -1, dst.dtype), dst, np.full(fill + 1, N, dst.dtype)])
    arrays = {
        "x": np.ascontiguousarray(x),
        "src": np.concatenate([src, np.zeros(fill, dst.dtype)]).reshape(P, T),
        "dst_window": np.ascontiguousarray(np.lib.stride_tricks.sliding_window_view(line, T + 2)[::T]),
        "edge_attr": np.concatenate([edge_attr_128, np.zeros((fill, F), np.float32)]),
        "edge_weight": np.concatenate([edge_weight1, np.zeros((fill, 1), np.float32)]).reshape(P, T),
        "W1": np.ascontiguousarray(L0_gnn_W1), "b1": np.ascontiguousarray(L0_gnn_b1),
        "W2": np.ascontiguousarray(L0_gnn_W2), "b2": np.ascontiguousarray(L0_gnn_b2),
        "Wa": np.ascontiguousarray(L0_gnn_Wa), "ba": np.ascontiguousarray(L0_gnn_ba),
    }
    nc = bacc.Bacc("TRN2", target_bir_lowering=False, num_devices=1)
    args = [nc.dram_tensor(n, a.shape, mybir.dt.from_np(a.dtype), kind="ExternalInput").ap()
            for n, a in arrays.items()]
    out = nc.dram_tensor("out", (N, F), F32, kind="ExternalOutput").ap()
    build(nc, *args, out)
    r = run_bass_kernel_spmd(nc, [arrays], core_ids=[0])
    return r.results[0]["out"]
```

```python
from contextlib import ExitStack

import concourse.bass as bass
from concourse import mybir
from concourse.alu_op_type import AluOpType as ALU

ACT = mybir.ActivationFunctionType
F32 = mybir.dt.float32
I32 = mybir.dt.int32
AX_X = mybir.AxisListType.X

P = 128
EPS = 1e-5
FAR = 1 << 20
G = 4
SETS = 4
SLOTS = 6
TRIO = 3
ROWS = 12
STATS = 6


def sizes(n_nodes, n_edges, f):
    tiles = -(-n_edges // P)
    assert tiles % G == 0 and f == P
    groups = tiles // G
    per_part = n_nodes // P
    chunks = per_part // ROWS
    rest = n_nodes - chunks * ROWS * P
    return tiles, groups, chunks * ROWS, chunks, rest


def build(nc, x, src, dstw, attr, conf, W1, b1, W2, b2, Wa, ba, out):
    N, F = x.shape
    T, GROUPS, PER, CHUNKS, REST = sizes(N, src.shape[0] * src.shape[1], F)
    REST_P = 32
    REST_R = REST // REST_P
    assert REST % REST_P == 0
    ITERS = min(GROUPS // SETS, CHUNKS // SLOTS)
    LAST_GROUPS = range(ITERS * SETS, GROUPS)
    LAST_CHUNKS = CHUNKS - ITERS * SLOTS
    assert len(LAST_GROUPS) == 2 * SETS + 1 and TRIO < LAST_CHUNKS <= SLOTS
    QUARTERS = [
        dict(load=1, stats=(0, 1, 2), scale=0),
        dict(stats=(3,), norm=0, before=(0,), after=(1, 2), store=0),
        dict(load=0, stats=(4, 5), scale=1),
        dict(norm=1, before=(3,), after=(4, 5), store=1),
    ]
    LAST_QUARTERS = [
        dict(load=1, stats=(0, 1, 2), scale=0),
        dict(stats=(3,), norm=0, before=(0,), after=(1, 2), store=0),
        dict(stats=(4, 5), scale=1, rest=True),
        dict(norm=1, before=(3,), after=(4, 5), store=1),
        dict(), dict(first=(0,)), dict(first=(1,)), dict(first=(2,)), dict(first=(3,)),
    ]
    ROOT = float(F) ** 0.5
    ACT_ROWS = 6
    ESTEPS = G
    SSTEPS = 15
    RSQRT_BITS = 0x5F3759DF

    with ExitStack() as ctx:
        def sb(name, shape, dt=F32):
            return ctx.enter_context(nc.sbuf_tensor(name, shape, dt))

        def psum(name, shape):
            return ctx.enter_context(nc.psum_tensor(name, shape, F32))

        def sem(name):
            return ctx.enter_context(nc.semaphore(name))

        def sems(name, n):
            return [sem(f"{name}{i}") for i in range(n)]

        ident = sb("ident", [P, P])
        w1 = sb("w1", [P, 3, F])
        b1_col = sb("b1_col", [P, 1])
        w2x = sb("w2x", [P, F + 1])
        b2x = sb("b2x", [1, F + 1])
        b2_col = sb("b2_col", [P, 1])
        wa_col = sb("wa_col", [P, 1])
        wa_conf = sb("wa_conf", [P, 1])
        ba_one = sb("ba_one", [1, 1])
        dst_win = sb("dst_win", [P, T + 2], I32)
        dst_f = sb("dst_f", [P, T + 2])
        gather_idx = sb("gather_idx", [P, GROUPS, 2 * G], I32)
        keep = sb("keep", [P, T])
        is_head = sb("is_head", [P, T])
        row_idx = sb("row_idx", [P, T], I32)
        logit_lin = sb("logit_lin", [P, T])
        small = sb("small", [P, 16])
        fall_sum = sb("fall_sum", [P, 1])
        ones_all = sb("ones_all", [P, P])
        fell = sb("fell", [P, 1])
        head_len = sb("head_len", [P, 1])
        head_most = sb("head_most", [1, 2])
        head_count = sb("head_count", [1, 1], I32)
        unsorted = sb("unsorted", [1, 1], I32)
        fix_idx = sb("fix_idx", [P, 2], I32)
        idx_slot = sb("idx_slot", [P, SETS, 2 * G], I32)
        rows = sb("rows", [P, SETS, 2 * G, F])
        attr_in = sb("attr_in", [P, SETS, G, F])
        turned = sb("turned", [P, 2, 3, G * P])
        hid = sb("hid", [P, 2, G * P])
        weight = sb("weight", [P, G])
        gated = sb("gated", [P, SETS, G, F])
        acc = sb("acc", [P, 2, G, F])
        head = sb("head", [P, F])
        e_stats = sb("e_stats", [P, G, STATS])
        e_sc = sb("e_sc", [P, SETS, 8, G])
        stash = sb("stash", [P, T, F])
        early = stash[:].rearrange("p t f -> p (t f)")
        src_idx = early[:, 0:T].bitcast(I32)
        skip = early[:, 256:256 + T]
        falls = early[:, 512:512 + T + 1]
        w2_turned = early[:, 768:768 + P]
        ridx_slot = sb("ridx_slot", [P, SETS, G], I32)
        any_dst = sb("any_dst", [P, 1])
        any_later = sb("any_later", [P, 1])
        any_get = sb("any_get", [P, 1], I32)
        any_put = sb("any_put", [P, 1], I32)
        nodes = sb("nodes", [P, SLOTS, ROWS, F])
        n_stats = sb("n_stats", [P, TRIO * ROWS, STATS])
        n_sc = sb("n_sc", [P, 2, 8, TRIO * ROWS])
        rest_in = sb("rest_in", [REST_P, REST_R, F])
        rest_stats = sb("rest_stats", [REST_P, REST_R, STATS])
        rest_sc = sb("rest_sc", [REST_P, 8, REST_R])
        fix_out = sb("fix_out", [P, F])
        fix_rows = sb("fix_rows", [P, F])
        match = sb("match", [P, P])
        upper = sb("upper", [P, P])
        r_stats = sb("r_stats", [P, STATS])
        r_sc = sb("r_sc", [P, 8, 1])

        messages = nc.dram_tensor("messages", (P, T, F), F32, kind="Internal").ap()
        sums_by_node = nc.dram_tensor("sums_by_node", (N, F), F32, kind="Internal").ap()

        turn_ps = psum("turn_ps", [P, 3, G * P])
        hid_ps = psum("hid_ps", [P, G * P])
        msg_ps = psum("msg_ps", [P, 2, 512])
        misc_ps = psum("misc_ps", [P, 512])

        def msg(j):
            return msg_ps[:, j // 2, (j % 2) * 256:(j % 2) * 256 + F + 1]

        consts_in = sem("consts_in")
        edges_in = sem("edges_in")
        pool_const = sem("pool_const")
        w2_in_ps = sem("w2_in_ps")
        w2_turned_ok = sem("w2_turned_ok")
        wa_in_ps = sem("wa_in_ps")
        w2_ready = sem("w2_ready")
        lin_ready = sem("lin_ready")
        prep = sem("prep")
        idx_ready = sems("idx_ready", SETS)
        gathered = sems("gathered", SETS)
        attr_landed = sems("attr_landed", SETS)
        turned_ps_ready = sem("turned_ps_ready")
        turned_ready = sem("turned_ready")
        hid_ps_ready = sem("hid_ps_ready")
        hid_ready = sem("hid_ready")
        msg_ready = sem("msg_ready")
        weight_ready = sem("weight_ready")
        gated_ready = sem("gated_ready")
        head_step = sem("head_step")
        head_groups_ready = sem("head_groups_ready")
        edge_step = sem("edge_step")
        rows_free = sems("rows_free", SETS)
        x_landed = sems("x_landed", SLOTS)
        node_stat = sem("node_stat")
        node_step = sem("node_step")
        scale_ready = sems("scale_ready", 2)
        act_normed = sems("act_normed", SLOTS)
        dve_normed = sems("dve_normed", SLOTS)
        stored = sems("stored", SLOTS)
        rest_landed = sem("rest_landed")
        rest_normed = sem("rest_normed")
        rest_stored = sem("rest_stored")
        e_stat = sem("e_stat")
        e_scale = sems("e_scale", SETS)
        final_step = sem("final_step")
        rest_step = sem("rest_step")
        rest_scale = sem("rest_scale")
        fix_step = sem("fix_step")
        ridx_ready = sems("ridx_ready", SETS)
        out_ready = sems("out_ready", SETS)
        scattered = sems("scattered", SETS)
        fix_idx_ready = sem("fix_idx_ready")
        fix_gathered = sem("fix_gathered")
        first_ps = sem("first_ps")
        match_ready = sem("match_ready")
        tails_ps = sem("tails_ps")
        fix_ready = sem("fix_ready")
        fix_scattered = sem("fix_scattered")

        saved = sems("saved", SETS)
        fall_ready = sem("fall_ready")
        fall_ps = sem("fall_ps")
        flag_ready = sem("flag_ready")
        any_start = sem("any_start")
        any_zeroed = sem("any_zeroed")
        any_cleared = sem("any_cleared")
        any_loaded = sem("any_loaded")
        any_dst_ready = sem("any_dst_ready")
        any_dst_ps = sem("any_dst_ps")
        any_same_step = sem("any_same_step")
        any_same_ready = sem("any_same_ready")
        any_sum_ps = sem("any_sum_ps")
        any_got = sem("any_got")
        any_new = sem("any_new")
        any_put_done = sem("any_put_done")
        all_idx_ready = sem("all_idx_ready")
        all_got = sem("all_got")
        all_step = sem("all_step")
        all_scale = sem("all_scale")
        all_ready = sem("all_ready")
        all_written = sem("all_written")

        block = ctx.enter_context(nc.Block())

        def wait(eng, semaphore, value):
            if not (isinstance(value, int) and value <= 0):
                eng.wait_ge(semaphore, value)

        def slots_in(it, slots):
            return [u for u in slots if not isinstance(it, int) or it * SLOTS + u < CHUNKS]

        def half(h):
            return range(h * TRIO, (h + 1) * TRIO)

        def every_quarter(eng, quarter):
            for s in range(SETS):
                quarter(0, s, **QUARTERS[s])
            with eng.Fori(1, ITERS) as it:
                for s in range(SETS):
                    quarter(it, s, **QUARTERS[s])
            for g in LAST_GROUPS:
                quarter(g // SETS, g % SETS, **LAST_QUARTERS[g - LAST_GROUPS[0]])

        def more(it, s, ahead):
            return not isinstance(it, int) or it * SETS + s + ahead < GROUPS

        attr_rows = attr.rearrange("(p t) f -> p t f", p=P)
        x_main = x[0:PER * P].rearrange("(p r) f -> p r f", p=P)
        out_main = out[0:PER * P].rearrange("(p r) f -> p r f", p=P)

        def chunk_of(view, c):
            return view[:, bass.ds(c * ROWS, ROWS), :]

        def tiles_of(t, g, n=G):
            return t[:, bass.ds(g * G, n)]

        @block.sync
        def _(sp):
            for dst, source in ((src_idx[:], src), (dst_win[:], dstw), (logit_lin[:], conf)):
                sp.dma_start(dst, source).then_inc(edges_in, 16)
            consts = [
                (w1[:], W1.rearrange("(c k) o -> k c o", c=3)),
                (b1_col[:], b1.rearrange("(o u) -> o u", u=1)),
                (w2x[:, 0:F], W2),
                (b2x[0:1, 0:F], b2.rearrange("(u o) -> u o", u=1)),
                (b2_col[:], b2.rearrange("(o u) -> o u", u=1)),
                (wa_col[:], Wa[0:F, :]),
                (wa_conf[:], Wa[F:F + 1, :].partition_broadcast(P)),
                (ba_one[:], ba.rearrange("(u o) -> u o", u=1)),
            ]
            for dst, source in consts:
                sp.dma_start(dst, source).then_inc(consts_in, 16)

            for s in range(SETS):
                sp.dma_start(attr_in[:, s], tiles_of(attr_rows, s)).then_inc(attr_landed[s], 16)
            for u in half(0):
                sp.dma_start(nodes[:, u], chunk_of(x_main, u)).then_inc(x_landed[u], 16)
            sp.dma_start(rest_in[:], x[PER * P:N, :].rearrange("(p r) f -> p r f", p=REST_P)
                         ).then_inc(rest_landed, 16)
            sp.wait_ge(flag_ready, 1)

            def load_nodes(c, u):
                sp.dma_start(nodes[:, u], chunk_of(x_main, c)).then_inc(x_landed[u], 16)

            def load_attr(g, s):
                sp.dma_start(attr_in[:, s], tiles_of(attr_rows, g)).then_inc(attr_landed[s], 16)

            def store_nodes(c, u, it):
                sp.wait_ge(act_normed[u], it + 1)
                sp.wait_ge(dve_normed[u], it + 1)
                sp.dma_start(chunk_of(out_main, c), nodes[:, u]).then_inc(stored[u], 16)

            is_unsorted = sp.value_load(unsorted[0:1, 0:1], min_val=0, max_val=1)

            def save_messages(it, s):
                with sp.If(is_unsorted > 0):
                    sp.wait_ge(gated_ready, G * (it * SETS + s + 1))
                    sp.dma_start(tiles_of(messages, it * SETS + s), gated[:, s]).then_inc(saved[s], 16)
                with sp.Else():
                    sp.sem_inc(saved[s], 16)

            def quarter(it, s, load=None, store=None, rest=False, **_):
                if more(it, s, SETS):
                    sp.wait_ge(turned_ps_ready, 3 * (it * SETS + s + 1))
                    load_attr(it * SETS + s + SETS, s)
                if load is not None:
                    to = it + 1 if load == 0 else it
                    for u in slots_in(to, half(load)):
                        wait(sp, stored[u], 16 * to)
                        load_nodes(to * SLOTS + u, u)
                save_messages(it, s)
                if store is not None:
                    for u in slots_in(it, half(store)):
                        store_nodes(it * SLOTS + u, u, it)
                if rest:
                    sp.wait_ge(rest_normed, 1)
                    sp.dma_start(out[PER * P:N, :].rearrange("(p r) f -> p r f", p=REST_P), rest_in[:]
                                 ).then_inc(rest_stored, 16)

            every_quarter(sp, quarter)

            def sort_out(sp):
                sp.wait_ge(any_start, 1)
                sp.wait_ge(any_zeroed, 1)
                zeros = nodes[:, SLOTS - 1]
                sums_main = sums_by_node[0:PER * P].rearrange("(p r) f -> p r f", p=P)
                with sp.Fori(0, CHUNKS) as c:
                    sp.dma_start(chunk_of(sums_main, c), zeros).then_inc(any_cleared, 16)
                sp.dma_start(sums_by_node[PER * P:N, :].rearrange("(p r) f -> p r f", p=REST_P),
                             nodes[0:REST_P, SLOTS - 1, 0:REST_R, :]).then_inc(any_cleared, 16)
                with sp.Fori(1, T + 1) as nth:
                    sp.wait_ge(any_start, nth)
                    sp.dma_start(gated[:, 0, 0, :], messages[:, bass.ds(nth - 1, 1), :].rearrange("p u f -> p (u f)")
                                 ).then_inc(any_loaded, 16)

            with sp.If(is_unsorted > 0):
                sort_out(sp)
            sp.nop()

        @block.gpsimd
        def _(pool):
            pool.memset(ident[:], 0.0).then_inc(pool_const, 1)
            pool.memset(head[:], 0.0).then_inc(pool_const, 1)
            pool.memset(acc[:], 0.0).then_inc(pool_const, 1)
            pool.memset(upper[:], 1.0).then_inc(pool_const, 1)
            pool.memset(ones_all[:], 1.0).then_inc(pool_const, 1)
            pool.wait_ge(pool_const, 5)
            pool.affine_select(out=upper[:], in_=upper[:], compare_op=ALU.is_gt, fill=0.0, base=0,
                               pattern=[[1, P]], channel_multiplier=-1).then_inc(pool_const, 1)
            pool.affine_select(out=ident[:], in_=ident[:], compare_op=ALU.not_equal, fill=1.0, base=0,
                               pattern=[[-1, P]], channel_multiplier=1).then_inc(pool_const, 1)

            def gather(nth, s):
                pool.wait_ge(pool_const, 7)
                pool.wait_ge(idx_ready[s], nth)
                pool.wait_ge(rows_free[s], nth)
                for j in range(2 * G):
                    pool.indirect_dma_start(
                        out=rows[:, s, j, :], out_offset=None, in_=x[:, :],
                        in_offset=bass.IndirectOffsetOnAxis(ap=idx_slot[:, s, j:j + 1], axis=0),
                    ).then_inc(gathered[s], 16)

            for s in range(SETS):
                pool.sem_inc(rows_free[s], 1)
            with pool.Fori(1, ITERS + 1) as nth:
                for s in range(SETS):
                    gather(nth, s)
            for g in LAST_GROUPS:
                gather(g // SETS + 1, g % SETS)
            pool.wait_ge(fix_idx_ready, 1)
            pool.indirect_dma_start(
                out=fix_rows[:, :], out_offset=None, in_=x[:, :],
                in_offset=bass.IndirectOffsetOnAxis(ap=fix_idx[:, 0:1], axis=0),
            ).then_inc(fix_gathered, 16)

            for u in range(SLOTS):
                pool.wait_ge(stored[u], 16 * len(range(u, CHUNKS, SLOTS)))
            pool.wait_ge(rest_stored, 16)

            def scatter(nth, s):
                pool.wait_ge(pool_const, 7)
                pool.wait_ge(out_ready[s], nth)
                pool.wait_ge(ridx_ready[s], nth)
                for j in range(G):
                    pool.indirect_dma_start(
                        out=out[:, :], out_offset=bass.IndirectOffsetOnAxis(ap=ridx_slot[:, s, j:j + 1], axis=0),
                        in_=nodes[:, s, j, :], in_offset=None, bounds_check=N - 1, oob_is_err=False,
                    ).then_inc(scattered[s], 16)

            with pool.Fori(1, GROUPS // SETS + 1) as nth:
                for s in range(SETS):
                    scatter(nth, s)
            for g in range(GROUPS // SETS * SETS, GROUPS):
                scatter(g // SETS + 1, g % SETS)
            pool.wait_ge(fix_ready, 1)
            pool.indirect_dma_start(
                out=out[:, :], out_offset=bass.IndirectOffsetOnAxis(ap=fix_idx[:, 1:2], axis=0),
                in_=fix_out[:, :], in_offset=None, bounds_check=N - 1, oob_is_err=False,
            ).then_inc(fix_scattered, 16)
            for s in range(SETS):
                pool.wait_ge(scattered[s], 16 * G * len(range(s, GROUPS, SETS)))
            pool.wait_ge(fix_scattered, 16)

            def get(to, table, idx, semaphore):
                pool.indirect_dma_start(
                    out=to, out_offset=None, in_=table[:, :],
                    in_offset=bass.IndirectOffsetOnAxis(ap=idx, axis=0)).then_inc(semaphore, 16)

            def put(table, idx, rows_, semaphore):
                pool.indirect_dma_start(
                    out=table[:, :], out_offset=bass.IndirectOffsetOnAxis(ap=idx, axis=0),
                    in_=rows_, in_offset=None, bounds_check=N - 1, oob_is_err=False).then_inc(semaphore, 16)

            def sort_out():
                for s in range(SETS):
                    pool.wait_ge(saved[s], 16 * len(range(s, GROUPS, SETS)))
                pool.sem_inc(any_start, 1)
                pool.wait_ge(any_cleared, 16 * (CHUNKS + 1))
                with pool.Fori(1, T + 1) as nth:
                    pool.wait_ge(pool_const, 7)
                    pool.wait_ge(any_same_ready, nth)
                    get(rows[:, 0, 0, :], sums_by_node, any_get[:, 0:1], any_got)
                    pool.wait_ge(pool_const, 7)
                    pool.wait_ge(any_new, nth)
                    put(sums_by_node, any_put[:, 0:1], rows[:, 0, 1, :], any_put_done)
                    pool.wait_ge(any_put_done, nth * 16)
                    pool.sem_inc(any_start, 1)
                with pool.Fori(1, T + 1) as nth:
                    pool.wait_ge(pool_const, 7)
                    pool.wait_ge(all_idx_ready, nth)
                    get(rows[:, 0, 0, :], sums_by_node, any_get[:, 0:1], all_got)
                    get(rows[:, 0, 1, :], x, any_get[:, 0:1], all_got)
                    pool.wait_ge(pool_const, 7)
                    pool.wait_ge(all_ready, nth)
                    put(out, any_put[:, 0:1], rows[:, 0, 3, :], all_written)
                pool.wait_ge(all_written, 16 * T)

            pool.wait_ge(flag_ready, 1)
            with pool.If(pool.value_load(unsorted[0:1, 0:1], min_val=0, max_val=1) > 0):
                sort_out()
            pool.nop()

        @block.scalar
        def _(act):
            def turn(it, s):
                g = it * SETS + s
                for c in range(3):
                    act.wait_ge(turned_ps_ready, 3 * g + c + 1)
                    if c == 0:
                        wait(act, hid_ps_ready, g - 1)
                    act.activation(turned[:, s % 2, c], turn_ps[:, c], ACT.Copy).then_inc(turned_ready, 1)

            def relu(it, s):
                g = it * SETS + s
                act.wait_ge(hid_ps_ready, g + 1)
                wait(act, msg_ready, g - 1)
                act.activation(hid[:, s % 2], hid_ps[:], ACT.Relu, bias=b1_col[:, 0:1]).then_inc(hid_ready, 1)

            def gates(it, s):
                g = it * SETS + s
                act.wait_ge(msg_ready, g + 1)
                wait(act, gated_ready, G * g)
                act.activation(weight[:].rearrange("p (a b) -> p a b", a=2), msg_ps[:, :, F:512:256],
                               ACT.Sigmoid).then_inc(weight_ready, 1)
                act.wait_ge(weight_ready, g + 1)
                act.wait_ge(rows_free[s], it + 1)
                wait(act, saved[s], 16 * it)
                for j in range(G):
                    act.activation(gated[:, s, j, :], msg(j)[:, 0:F], ACT.Copy,
                                   scale=weight[:, j:j + 1]).then_inc(gated_ready, 1)

            def norm(it, u):
                h = u // TRIO
                act.wait_ge(scale_ready[h], 2 * (it + 1))
                for r in range(ACT_ROWS):
                    k = (u % TRIO) * ROWS + r
                    last = act.activation(nodes[:, u, r, :], nodes[:, u, r, :], ACT.Identity,
                                          scale=n_sc[:, h, 6, k:k + 1], bias=n_sc[:, h, 7, k:k + 1])
                last.then_inc(act_normed[u], 1)

            def finish(it, s):
                g = it * SETS + s
                wait(act, scattered[s], 16 * G * it)
                act.wait_ge(e_scale[s], 2 * (it + 1))
                for j in range(G):
                    last = act.activation(nodes[:, s, j, :], stash[:, bass.ds(g * G + j, 1), :].rearrange("p u f -> p (u f)"),
                                          ACT.Identity, scale=e_sc[:, s, 6, j:j + 1], bias=e_sc[:, s, 7, j:j + 1])
                last.then_inc(out_ready[s], 1)

            def quarter(it, s, before=(), after=(), first=(), **_):
                relu(it, s)
                if more(it, s, 1):
                    turn(it + (s + 1) // SETS, (s + 1) % SETS)
                for u in slots_in(it, before):
                    norm(it, u)
                gates(it, s)
                for u in slots_in(it, after):
                    norm(it, u)
                finish_first(first)

            def finish_first(some):
                for s in some:
                    act.wait_ge(stored[s], 16 * len(range(s, CHUNKS, SLOTS)))
                    finish(0, s)

            act.wait_ge(consts_in, 16 * 8)
            turn(0, 0)
            every_quarter(act, quarter)
            with act.Fori(1, GROUPS // SETS) as it:
                for s in range(SETS):
                    finish(it, s)
            for g in range(GROUPS // SETS * SETS, GROUPS):
                finish(g // SETS, g % SETS)

        @block.tensor
        def _(pe):
            pe.wait_ge(pool_const, 7)
            pe.wait_ge(fall_ready, 2)
            pe.matmul(hid_ps[0:1, P:2 * P], head_len[:], ident[:], start=True, stop=True)
            pe.matmul(hid_ps[:, 0:1], ones_all[:], fall_sum[:], start=True, stop=True).then_inc(fall_ps, 1)
            pe.wait_ge(consts_in, 16 * 8)
            pe.wait_ge(flag_ready, 1)
            pe.transpose(misc_ps[:, 0:P], w2x[:, 0:F], ident[:]).then_inc(w2_in_ps, 1)
            pe.wait_ge(w2_turned_ok, 1)
            pe.matmul(misc_ps[:, 256:257], w2_turned[:], wa_col[:], start=True, stop=True)
            pe.matmul(misc_ps[0:1, 260:261], b2_col[:], wa_col[:], start=True, stop=True).then_inc(wa_in_ps, 1)

            def turn(it, s):
                g = it * SETS + s
                pe.wait_ge(gathered[s], 16 * 2 * G * (it + 1))
                pe.wait_ge(attr_landed[s], 16 * (it + 1))
                wait(pe, turned_ready, 3 * g)
                for c in range(3):
                    for j in range(G):
                        tile = attr_in[:, s, j, :] if c == 2 else rows[:, s, c * G + j, :]
                        last = pe.transpose(turn_ps[:, c, j * P:(j + 1) * P], tile, ident[:])
                    last.then_inc(turned_ps_ready, 1)

            def quarter(it, s, **_):
                g = it * SETS + s
                pe.wait_ge(turned_ready, 3 * g + 3)
                wait(pe, hid_ready, g)
                for c in range(3):
                    last = pe.matmul(hid_ps[:], w1[:, c, :], turned[:, s % 2, c, :], start=(c == 0), stop=(c == 2))
                last.then_inc(hid_ps_ready, 1)
                if more(it, s, 1):
                    turn(it + (s + 1) // SETS, (s + 1) % SETS)
                pe.wait_ge(hid_ready, g + 1)
                wait(pe, gated_ready, G * g)
                for j in range(G):
                    pe.matmul(msg(j), hid[:, s % 2, j * P:(j + 1) * P], w2x[:], start=True, stop=False)
                    pe.matmul(msg(j), ones_all[0:1, :], b2x[:], start=False, stop=False)
                    last = pe.matmul(msg(j)[:, F:F + 1], ident[:], logit_lin[:, bass.ds(g * G + j, 1)],
                                     start=False, stop=True)
                last.then_inc(msg_ready, 1)

            turn(0, 0)
            pe.wait_ge(w2_ready, 2)
            pe.wait_ge(lin_ready, 1)
            every_quarter(pe, quarter)

            pe.wait_ge(prep, 1)
            pe.matmul(misc_ps[:, 0:P], dst_f[:, 1:2].to_broadcast([P, P]), ident[:], start=True,
                      stop=True).then_inc(first_ps, 1)
            pe.wait_ge(match_ready, 1)
            lg = LAST_GROUPS[-1]
            pe.wait_ge(edge_step, ESTEPS * (lg + 1))
            pe.matmul(misc_ps[:, 0:P], match[:], acc[:, lg % 2, G - 1, :], start=True,
                      stop=True).then_inc(tails_ps, 1)

            def sort_out():
                pe.wait_ge(fix_ready, 1)
                with pe.Fori(1, T + 1) as nth:
                    pe.wait_ge(any_dst_ready, nth)
                    pe.matmul(misc_ps[:, 0:P], any_dst[:, 0:1].to_broadcast([P, P]), ident[:], start=True,
                              stop=True).then_inc(any_dst_ps, 1)
                    pe.wait_ge(any_same_ready, nth)
                    pe.wait_ge(any_loaded, nth * 16)
                    pe.matmul(hid_ps[:, 0:P], match[:], gated[:, 0, 0, :], start=True,
                              stop=True).then_inc(any_sum_ps, 1)

            with pe.If(pe.value_load(unsorted[0:1, 0:1], min_val=0, max_val=1) > 0):
                sort_out()
            pe.nop()

        @block.vector
        def _(dve):
            done = [0]

            def step(ins):
                done[0] += 1
                ins.then_inc(prep, 1)

            def settle():
                dve.wait_ge(prep, done[0])

            dve.wait_ge(edges_in, 16 * 3)
            d, before, after = dst_f[:, 1:T + 1], dst_f[:, 0:T], dst_f[:, 2:T + 2]
            step(dve.tensor_copy(dst_f[:], dst_win[:]))
            step(dve.tensor_copy(gather_idx[:, :, 0:G], src_idx[:].rearrange("p (g j) -> p g j", j=G)))
            settle()
            step(dve.tensor_scalar(gather_idx[:, :, G:2 * G], dst_f[:, 1:T + 1].rearrange("p (g j) -> p g j", j=G),
                                   float(N - 1), None, ALU.min))
            settle()
            for s in range(SETS):
                dve.tensor_copy(idx_slot[:, s], gather_idx[:, s]).then_inc(idx_ready[s], 1)
            step(dve.tensor_tensor(keep[:], d, before, ALU.is_equal))
            step(dve.tensor_scalar(is_head[:], d, dst_f[:, 0:1], None, ALU.is_equal))
            step(dve.tensor_tensor(skip[:], d, after, ALU.is_equal))
            step(dve.tensor_tensor(falls[:], dst_f[:, 0:T + 1], dst_f[:, 1:T + 2], ALU.is_gt))
            settle()
            step(dve.memset(keep[:, 0:1], 0.0))
            dve.tensor_reduce(fall_sum[:], falls[:], AX_X, ALU.add).then_inc(fall_ready, 1)
            dve.tensor_reduce(head_len[:], is_head[:], AX_X, ALU.add).then_inc(fall_ready, 1)
            step(dve.tensor_tensor(skip[:], skip[:], is_head[:], ALU.add))
            dve.wait_ge(fall_ps, 1)
            step(dve.tensor_scalar(fell[:], hid_ps[:, 0:1], 1.0, None, ALU.min))
            step(dve.tensor_reduce(head_most[:, 0:1], hid_ps[0:1, P:2 * P], AX_X, ALU.max))
            settle()
            step(dve.tensor_scalar(head_most[:, 1:2], head_most[:, 0:1], 1.0 / G, 1.0, ALU.mult, ALU.add))
            settle()
            dve.tensor_scalar(head_count[:], head_most[:, 1:2], float(SETS), float(GROUPS), ALU.max, ALU.min
                              ).then_inc(head_groups_ready, 1)
            dve.tensor_copy(unsorted[:], fell[0:1, :]).then_inc(flag_ready, 1)
            step(dve.tensor_scalar(skip[:], skip[:], fell[:, 0:1], None, ALU.add))
            settle()
            step(dve.scalar_tensor_tensor(row_idx[:], skip[:], float(FAR), d, ALU.mult, ALU.add))
            first, last_, prev, nxt = dst_f[:, 1:2], dst_f[:, T:T + 1], dst_f[:, 0:1], dst_f[:, T + 1:T + 2]
            step(dve.tensor_tensor(small[:, 0:1], first, prev, ALU.is_equal))
            step(dve.tensor_tensor(small[:, 1:2], first, last_, ALU.is_equal))
            step(dve.tensor_tensor(small[:, 2:3], nxt, last_, ALU.is_equal))
            settle()
            step(dve.tensor_tensor(small[:, 3:4], small[:, 1:2], small[:, 2:3], ALU.mult))
            settle()
            step(dve.tensor_scalar(small[:, 4:5], small[:, 3:4], -1.0, 1.0, ALU.mult, ALU.add))
            settle()
            step(dve.tensor_tensor(small[:, 5:6], small[:, 4:5], small[:, 0:1], ALU.mult))
            settle()
            step(dve.tensor_tensor(small[:, 5:6], small[:, 5:6], fell[:], ALU.is_gt))
            settle()
            step(dve.tensor_scalar(small[:, 6:7], small[:, 5:6], -float(FAR), float(FAR), ALU.mult, ALU.add))
            settle()
            step(dve.tensor_tensor(fix_idx[:, 1:2], small[:, 6:7], first, ALU.add))
            settle()
            dve.tensor_copy(fix_idx[:, 0:1], first).then_inc(fix_idx_ready, 1)
            dve.wait_ge(consts_in, 16 * 8)
            dve.tensor_scalar(logit_lin[:], logit_lin[:], wa_conf[:, 0:1], None, ALU.mult).then_inc(lin_ready, 1)
            dve.wait_ge(w2_in_ps, 1)
            dve.tensor_copy(w2_turned[:], misc_ps[:, 0:P]).then_inc(w2_turned_ok, 1)
            dve.wait_ge(wa_in_ps, 1)
            dve.tensor_copy(w2x[:, F:F + 1], misc_ps[:, 256:257]).then_inc(w2_ready, 1)
            dve.tensor_tensor(b2x[0:1, F:F + 1], misc_ps[0:1, 260:261], ba_one[:], ALU.add).then_inc(w2_ready, 1)
            settle()
            dve.wait_ge(pool_const, 7)

            def scales(st, sc, sem_, base, final):
                mean_e, m2_e, mean_o, m2_o = (st[:, :, k] for k in (1, 2, 4, 5))
                mean2, apart, v, y, a = (sc[:, k] for k in range(5))
                n = [0]

                def then(ins, wait=True):
                    n[0] += 1
                    ins.then_inc(sem_, 1)
                    if wait:
                        dve.wait_ge(sem_, base + n[0])

                then(dve.tensor_tensor(mean2, mean_e, mean_o, ALU.add), False)
                then(dve.tensor_tensor(apart, mean_e, mean_o, ALU.subtract), False)
                then(dve.tensor_tensor(v, m2_e, m2_o, ALU.add))
                then(dve.scalar_tensor_tensor(a, apart, F / 4.0, apart, ALU.mult, ALU.mult))
                then(dve.scalar_tensor_tensor(v, v, F * EPS, a, ALU.add, ALU.add))
                then(dve.tensor_scalar(y.bitcast(I32), v.bitcast(I32), -0.5, float(RSQRT_BITS), ALU.mult, ALU.add))
                for three in (3.0, 12.0, 768.0):
                    then(dve.tensor_tensor(a, y, y, ALU.mult))
                    then(dve.tensor_tensor(a, a, v, ALU.mult))
                    then(dve.scalar_tensor_tensor(y, a, -three, y, ALU.add, ALU.mult))
                dve.tensor_scalar(sc[:, 6], y, -ROOT / 8192, None, ALU.mult).then_inc(final, 1)
                dve.scalar_tensor_tensor(sc[:, 7], mean2, 0.5 * ROOT / 8192, y, ALU.mult, ALU.mult).then_inc(final, 1)
                assert n[0] == SSTEPS

            def node_stats(it, u):
                dve.wait_ge(x_landed[u], 16 * (it + 1))
                for r in range(ROWS):
                    last = dve.bn_stats(n_stats[:, (u % TRIO) * ROWS + r, :], nodes[:, u, r, :])
                last.then_inc(node_stat, 1)

            def node_scales(it, h):
                n = len(slots_in(it, half(h)))
                before = min(CHUNKS, it * SLOTS + h * TRIO) if isinstance(it, int) else it * SLOTS + h * TRIO
                dve.wait_ge(node_stat, before + n)
                scales(n_stats[:, 0:n * ROWS], n_sc[:, h, :, 0:n * ROWS], node_step, SSTEPS * (2 * it + h),
                       scale_ready[h])

            def node_norm(it, u):
                h = u // TRIO
                dve.wait_ge(scale_ready[h], 2 * (it + 1))
                for r in range(ACT_ROWS, ROWS):
                    k = (u % TRIO) * ROWS + r
                    last = dve.tensor_scalar(nodes[:, u, r, :], nodes[:, u, r, :], n_sc[:, h, 6, k:k + 1],
                                             n_sc[:, h, 7, k:k + 1], ALU.mult, ALU.add)
                last.then_inc(dve_normed[u], 1)

            def next_indices(it, s):
                dve.wait_ge(gathered[s], 16 * 2 * G * (it + 1))
                dve.tensor_copy(idx_slot[:, s], gather_idx[:, bass.ds((it + 1) * SETS + s, 1), :]
                                .rearrange("p u j -> p (u j)")).then_inc(idx_ready[s], 1)

            def heads(it, s):
                for j in range(G):
                    t = (it * SETS + s) * G + j
                    dve.wait_ge(gated_ready, t + 1)
                    wait(dve, head_step, t)
                    dve.scalar_tensor_tensor(head[:], gated[:, s, j, :], is_head[:, bass.ds(t, 1)],
                                             head[:], ALU.mult, ALU.add).then_inc(head_step, 1)

            dve.wait_ge(head_groups_ready, 1)
            head_groups = dve.value_load(head_count[0:1, 0:1], min_val=SETS, max_val=GROUPS)

            def sums(it, s):
                g = it * SETS + s
                base = ESTEPS * g
                b = s % 2
                if isinstance(it, int) and it == 0:
                    heads(it, s)
                else:
                    with dve.If(head_groups > g):
                        heads(it, s)
                wait(dve, edge_step, base)
                for j in range(G):
                    t = g * G + j
                    prev_acc = acc[:, b, j - 1, :] if j else acc[:, 1 - b, G - 1, :]
                    dve.wait_ge(gated_ready, t + 1)
                    if j:
                        dve.wait_ge(edge_step, base + j)
                    dve.scalar_tensor_tensor(acc[:, b, j, :], prev_acc, keep[:, bass.ds(t, 1)],
                                             gated[:, s, j, :], ALU.mult, ALU.add).then_inc(edge_step, 1)
                dve.wait_ge(edge_step, base + G)
                dve.tensor_tensor(tiles_of(stash, g), acc[:, b], rows[:, s, G:2 * G, :], ALU.add
                                  ).then_inc(rows_free[s], 1)

            def finish(it, s):
                g = it * SETS + s
                wait(dve, scattered[s], 16 * G * it)
                dve.tensor_copy(ridx_slot[:, s], tiles_of(row_idx, g)).then_inc(ridx_ready[s], 1)
                dve.wait_ge(rows_free[s], it + 2)
                for j in range(G):
                    last = dve.bn_stats(e_stats[:, j, :], stash[:, bass.ds(g * G + j, 1), :].rearrange("p u f -> p (u f)"))
                last.then_inc(e_stat, 1)
                dve.wait_ge(e_stat, g + 1)
                wait(dve, out_ready[s], it)
                scales(e_stats[:], e_sc[:, s], final_step, SSTEPS * g, e_scale[s])

            def last_nodes():
                dve.wait_ge(rest_landed, 16)
                for r in range(REST_R):
                    last = dve.bn_stats(rest_stats[:, r, :], rest_in[:, r, :])
                last.then_inc(rest_step, 1)
                dve.wait_ge(rest_step, 1)
                scales(rest_stats[:], rest_sc[:], rest_step, 1, rest_scale)
                dve.wait_ge(rest_scale, 2)
                for r in range(REST_R):
                    last = dve.tensor_scalar(rest_in[:, r, :], rest_in[:, r, :], rest_sc[:, 6, r:r + 1],
                                             rest_sc[:, 7, r:r + 1], ALU.mult, ALU.add)
                last.then_inc(rest_normed, 1)

            def quarter(it, s, stats=(), scale=None, norm=None, first=(), rest=False, **_):
                if more(it, s, SETS):
                    next_indices(it, s)
                if norm is not None:
                    for u in slots_in(it, half(norm)):
                        node_norm(it, u)
                for u in slots_in(it, stats):
                    node_stats(it, u)
                if scale is not None:
                    node_scales(it, scale)
                if rest:
                    last_nodes()
                for k in first:
                    finish(0, k)
                sums(it, s)

            every_quarter(dve, quarter)

            dve.wait_ge(first_ps, 1)
            dve.tensor_scalar(match[:], misc_ps[:, 0:P], last_, None, ALU.is_equal).then_inc(fix_step, 1)
            dve.wait_ge(fix_step, 1)
            dve.tensor_tensor(match[:], match[:], upper[:], ALU.mult).then_inc(match_ready, 1)
            dve.wait_ge(fix_gathered, 16)
            dve.wait_ge(head_step, head_groups * G)
            dve.tensor_tensor(fix_rows[:], fix_rows[:], head[:], ALU.add).then_inc(fix_step, 1)
            dve.wait_ge(fix_step, 2)
            dve.wait_ge(tails_ps, 1)
            dve.tensor_tensor(fix_rows[:], fix_rows[:], misc_ps[:, 0:P], ALU.add).then_inc(fix_step, 1)
            dve.wait_ge(fix_step, 3)
            dve.bn_stats(r_stats[:, :], fix_rows[:, :]).then_inc(rest_step, 1)
            dve.wait_ge(rest_step, SSTEPS + 2)
            scales(r_stats[:].rearrange("p (u k) -> p u k", u=1), r_sc[:], rest_step, SSTEPS + 2, rest_scale)
            dve.wait_ge(rest_scale, 4)
            dve.tensor_scalar(fix_out[:], fix_rows[:], r_sc[:, 6, :], r_sc[:, 7, :],
                              ALU.mult, ALU.add).then_inc(fix_ready, 1)

            with dve.Fori(1, GROUPS // SETS) as it:
                for s in range(SETS):
                    finish(it, s)
            for g in range(GROUPS // SETS * SETS, GROUPS):
                finish(g // SETS, g % SETS)

            def sort_out():
                dve.wait_ge(any_start, 1)
                dve.memset(nodes[:, SLOTS - 1], 0.0).then_inc(any_zeroed, 1)
                with dve.Fori(1, T + 1) as nth:
                    dve.wait_ge(any_start, nth)
                    dst_of = dst_f[:, bass.ds(nth, 1)]
                    dve.tensor_copy(any_dst[:], dst_of).then_inc(any_dst_ready, 1)
                    dve.tensor_scalar(any_get[:], dst_of, float(N - 1), None, ALU.min).then_inc(any_same_step, 1)
                    dve.wait_ge(any_dst_ready, nth)
                    dve.wait_ge(any_dst_ps, nth)
                    dve.tensor_scalar(match[:], misc_ps[:, 0:P], any_dst[:, 0:1], None, ALU.is_equal
                                      ).then_inc(any_same_step, 1)
                    dve.wait_ge(any_same_step, nth * 5 - 3)
                    dve.tensor_tensor(fix_out[:], match[:], upper[:], ALU.mult).then_inc(any_same_step, 1)
                    dve.wait_ge(any_same_step, nth * 5 - 2)
                    dve.tensor_reduce(any_later[:], fix_out[:], AX_X, ALU.add).then_inc(any_same_step, 1)
                    dve.wait_ge(any_same_step, nth * 5 - 1)
                    dve.scalar_tensor_tensor(any_put[:], any_later[:], float(FAR), any_dst[:], ALU.mult, ALU.add
                                             ).then_inc(any_same_step, 1)
                    dve.wait_ge(any_same_step, nth * 5)
                    dve.tensor_copy(row_idx[:, bass.ds(nth - 1, 1)], any_put[:]).then_inc(any_same_ready, 1)
                    dve.wait_ge(any_got, nth * 16)
                    dve.wait_ge(any_sum_ps, nth)
                    dve.tensor_tensor(rows[:, 0, 1, :], rows[:, 0, 0, :], hid_ps[:, 0:P], ALU.add).then_inc(any_new, 1)
                dve.wait_ge(any_start, T + 1)
                with dve.Fori(1, T + 1) as nth:
                    dve.tensor_scalar(any_get[:], dst_f[:, bass.ds(nth, 1)], float(N - 1), None, ALU.min
                                      ).then_inc(all_step, 1)
                    dve.wait_ge(all_step, nth * (SSTEPS + 3) - (SSTEPS + 2))
                    dve.tensor_copy(any_put[:], row_idx[:, bass.ds(nth - 1, 1)]).then_inc(all_idx_ready, 1)
                    dve.wait_ge(all_got, nth * 32)
                    dve.tensor_tensor(rows[:, 0, 2, :], rows[:, 0, 0, :], rows[:, 0, 1, :], ALU.add).then_inc(all_step, 1)
                    dve.wait_ge(all_step, nth * (SSTEPS + 3) - (SSTEPS + 1))
                    dve.bn_stats(r_stats[:], rows[:, 0, 2, :]).then_inc(all_step, 1)
                    dve.wait_ge(all_step, nth * (SSTEPS + 3) - SSTEPS)
                    scales(r_stats[:].rearrange("p (u k) -> p u k", u=1), r_sc[:], all_step,
                           nth * (SSTEPS + 3) - SSTEPS, all_scale)
                    dve.wait_ge(all_scale, nth * 2)
                    dve.tensor_scalar(rows[:, 0, 3, :], rows[:, 0, 2, :], r_sc[:, 6, :], r_sc[:, 7, :],
                                      ALU.mult, ALU.add).then_inc(all_ready, 1)
                    dve.wait_ge(all_written, nth * 16)

            dve.wait_ge(flag_ready, 1)
            with dve.If(dve.value_load(unsorted[0:1, 0:1], min_val=0, max_val=1) > 0):
                sort_out()
            dve.engine_nop()


def kernel(x, src, dst, edge_attr_128, edge_weight1, L0_gnn_W1, L0_gnn_b1, L0_gnn_W2, L0_gnn_b2, L0_gnn_Wa,
           L0_gnn_ba):
    import numpy as np
    import concourse.bacc as bacc
    from concourse.bass_utils import run_bass_kernel_spmd

    N, F = x.shape
    E = src.shape[0]
    T = -(-E // (P * G)) * G
    fill = P * T - E
    dst = np.ascontiguousarray(dst)
    line = np.concatenate([np.full(1, -1, dst.dtype), dst, np.full(fill + 1, N, dst.dtype)])
    arrays = {
        "x": np.ascontiguousarray(x),
        "src": np.concatenate([src, np.zeros(fill, dst.dtype)]).reshape(P, T),
        "dst_window": np.ascontiguousarray(np.lib.stride_tricks.sliding_window_view(line, T + 2)[::T]),
        "edge_attr": np.concatenate([edge_attr_128, np.zeros((fill, F), np.float32)]),
        "edge_weight": np.concatenate([edge_weight1, np.zeros((fill, 1), np.float32)]).reshape(P, T),
        "W1": np.ascontiguousarray(L0_gnn_W1), "b1": np.ascontiguousarray(L0_gnn_b1),
        "W2": np.ascontiguousarray(L0_gnn_W2), "b2": np.ascontiguousarray(L0_gnn_b2),
        "Wa": np.ascontiguousarray(L0_gnn_Wa), "ba": np.ascontiguousarray(L0_gnn_ba),
    }
    nc = bacc.Bacc("TRN2", target_bir_lowering=False, num_devices=1)
    args = [nc.dram_tensor(n, a.shape, mybir.dt.from_np(a.dtype), kind="ExternalInput").ap()
            for n, a in arrays.items()]
    out = nc.dram_tensor("out", (N, F), F32, kind="ExternalOutput").ap()
    build(nc, *args, out)
    r = run_bass_kernel_spmd(nc, [arrays], core_ids=[0])
    return r.results[0]["out"]
```

```python
from contextlib import ExitStack

import concourse.bass as bass
from concourse import mybir
from concourse.alu_op_type import AluOpType as ALU

ACT = mybir.ActivationFunctionType
F32 = mybir.dt.float32
I32 = mybir.dt.int32
AX_X = mybir.AxisListType.X

P = 128
EPS = 1e-5
FAR = 1 << 20
G = 4
SETS = 4
SLOTS = 6
TRIO = 3
ROWS = 11
STATS = 6


def sizes(n_nodes, n_edges, f):
    tiles = -(-n_edges // P)
    assert tiles % G == 0 and f == P
    groups = tiles // G
    per_part = n_nodes // P
    chunks = per_part // ROWS
    rest = n_nodes - chunks * ROWS * P
    return tiles, groups, chunks * ROWS, chunks, rest


def build(nc, x, src, dstw, attr, conf, W1, b1, W2, b2, Wa, ba, out):
    N, F = x.shape
    T, GROUPS, PER, CHUNKS, REST = sizes(N, src.shape[0] * src.shape[1], F)
    REST_P = 32
    REST_R = REST // REST_P
    assert REST > 0 and REST % REST_P == 0
    ITERS = min(GROUPS // SETS, CHUNKS // SLOTS)
    LAST_GROUPS = range(ITERS * SETS, GROUPS)
    LAST_CHUNKS = CHUNKS - ITERS * SLOTS
    assert len(LAST_GROUPS) == SETS + 1 and GROUPS % SETS == 1 and TRIO < LAST_CHUNKS <= SLOTS
    QUARTERS = [
        dict(stats=(0, 1, 2), scale=0, late_before=(5,), late_store=(5,), load=1),
        dict(stats=(3,), norm=0, before=(0,), after=(1,), store=(0, 1)),
        dict(stats=(4, 5), scale=1, before=(2,), store=(2,), load=0),
        dict(norm=1, before=(3,), after=(4,), store=(3, 4)),
    ]
    LAST_QUARTERS = [
        dict(QUARTERS[0]),
        dict(stats=(3, 4), scale=1, norm=0, before=(0,), after=(1, 2), store=(0, 1, 2)),
        dict(norm=1, before=(3, 4), store=(3, 4), first_scales=0),
        dict(first_scales=1, first=(0, 1)),
        dict(first=(2, 3)),
    ]
    ROOT = float(F) ** 0.5
    ACT_ROWS = (6, 7, 6, 6, 7, 6)
    LAST_ACT_ROWS = 5
    BESIDE = 8
    ESTEPS = G
    SSTEPS = 13
    RSQRT_BITS = 0x5F3759DF

    with ExitStack() as ctx:
        def sb(name, shape, dt=F32):
            return ctx.enter_context(nc.sbuf_tensor(name, shape, dt))

        def psum(name, shape):
            return ctx.enter_context(nc.psum_tensor(name, shape, F32))

        def sem(name):
            return ctx.enter_context(nc.semaphore(name))

        def sems(name, n):
            return [sem(f"{name}{i}") for i in range(n)]

        ident = sb("ident", [P, P])
        w1 = sb("w1", [P, 3, F])
        b1_col = sb("b1_col", [P, 1])
        w2x = sb("w2x", [P, F + 1])
        b2x = sb("b2x", [1, F + 1])
        b2_col = sb("b2_col", [P, 1])
        wa_col = sb("wa_col", [P, 1])
        wa_conf = sb("wa_conf", [P, 1])
        ba_one = sb("ba_one", [1, 1])
        dst_win = sb("dst_win", [P, T + 2], I32)
        dst_f = sb("dst_f", [P, T + 2])
        gather_idx = sb("gather_idx", [P, GROUPS, 2 * G], I32)
        keep = sb("keep", [P, T])
        is_head = sb("is_head", [P, T])
        row_idx = sb("row_idx", [P, T], I32)
        logit_lin = sb("logit_lin", [P, T])
        small = sb("small", [P, 16])
        fall_sum = sb("fall_sum", [P, 1])
        ones_all = sb("ones_all", [P, P])
        fell = sb("fell", [P, 1])
        head_len = sb("head_len", [P, 1])
        head_most = sb("head_most", [1, 2])
        head_count = sb("head_count", [1, 1], I32)
        unsorted = sb("unsorted", [1, 1], I32)
        fix_idx = sb("fix_idx", [P, 2], I32)
        idx_slot = sb("idx_slot", [P, SETS, 2 * G], I32)
        rows = sb("rows", [P, SETS, 2 * G, F])
        attr_in = sb("attr_in", [P, SETS, G, F])
        turned = sb("turned", [P, 2, 3, G * P])
        hid = sb("hid", [P, 2, G * P])
        weight = sb("weight", [P, G])
        gated = sb("gated", [P, SETS, G, F])
        acc = sb("acc", [P, 2, G, F])
        head = sb("head", [P, F])
        e_stats = sb("e_stats", [P, 2, G, STATS])
        e_sc = sb("e_sc", [P, SETS // 2, 8, 2, G])
        stash = sb("stash", [P, T, F])
        early = stash[:].rearrange("p t f -> p (t f)")
        src_idx = early[:, 0:T].bitcast(I32)
        skip = early[:, 256:256 + T]
        falls = early[:, 512:512 + T + 1]
        w2_turned = early[:, 768:768 + P]
        ridx_slot = sb("ridx_slot", [P, SETS, G], I32)
        any_dst = sb("any_dst", [P, 1])
        any_later = sb("any_later", [P, 1])
        any_get = sb("any_get", [P, 1], I32)
        any_put = sb("any_put", [P, 1], I32)
        nodes = sb("nodes", [P, SLOTS, ROWS, F])
        n_stats = sb("n_stats", [P, TRIO * ROWS, STATS])
        n_sc = sb("n_sc", [P, 2, 8, TRIO * ROWS])
        rest_in = sb("rest_in", [REST_P, REST_R, F])
        rest_stats = sb("rest_stats", [REST_P, REST_R, STATS])
        rest_sc = sb("rest_sc", [REST_P, 8, REST_R])
        fix_out = sb("fix_out", [P, F])
        fix_rows = sb("fix_rows", [P, F])
        match = sb("match", [P, P])
        upper = sb("upper", [P, P])
        r_stats = sb("r_stats", [P, STATS])
        r_sc = sb("r_sc", [P, 8, 1])

        messages = nc.dram_tensor("messages", (P, T, F), F32, kind="Internal").ap()
        sums_by_node = nc.dram_tensor("sums_by_node", (N, F), F32, kind="Internal").ap()

        turn_ps = psum("turn_ps", [P, 3, G * P])
        hid_ps = psum("hid_ps", [P, G * P])
        msg_ps = psum("msg_ps", [P, 2, 512])
        misc_ps = psum("misc_ps", [P, 512])

        def msg(j):
            return msg_ps[:, j // 2, (j % 2) * 256:(j % 2) * 256 + F + 1]

        consts_in = sem("consts_in")
        edges_in = sem("edges_in")
        pool_const = sem("pool_const")
        w2_in_ps = sem("w2_in_ps")
        w2_turned_ok = sem("w2_turned_ok")
        wa_in_ps = sem("wa_in_ps")
        w2_ready = sem("w2_ready")
        lin_ready = sem("lin_ready")
        prep = sem("prep")
        idx_ready = sems("idx_ready", SETS)
        gathered = sems("gathered", SETS)
        attr_landed = sems("attr_landed", SETS)
        turned_ps_ready = sem("turned_ps_ready")
        turned_ready = sem("turned_ready")
        hid_ps_ready = sem("hid_ps_ready")
        hid_ready = sem("hid_ready")
        msg_ready = sem("msg_ready")
        weight_ready = sem("weight_ready")
        gated_ready = sem("gated_ready")
        head_step = sem("head_step")
        head_groups_ready = sem("head_groups_ready")
        edge_step = sem("edge_step")
        src_free = sems("src_free", SETS)
        rows_free = sems("rows_free", SETS)
        x_landed = sems("x_landed", SLOTS)
        node_stat = sem("node_stat")
        node_step = sem("node_step")
        scale_ready = sems("scale_ready", 2)
        act_normed = sems("act_normed", SLOTS)
        dve_normed = sems("dve_normed", SLOTS)
        stored = sems("stored", SLOTS)
        rest_landed = sem("rest_landed")
        rest_normed = sem("rest_normed")
        rest_stored = sem("rest_stored")
        e_stat = sem("e_stat")
        e_scale = sems("e_scale", SETS // 2)
        final_step = sem("final_step")
        rest_step = sem("rest_step")
        rest_scale = sem("rest_scale")
        fix_step = sem("fix_step")
        ridx_ready = sems("ridx_ready", SETS)
        out_ready = sems("out_ready", SETS)
        scattered = sems("scattered", SETS)
        fix_idx_ready = sem("fix_idx_ready")
        fix_gathered = sem("fix_gathered")
        first_ps = sem("first_ps")
        match_ready = sem("match_ready")
        tails_ps = sem("tails_ps")
        fix_ready = sem("fix_ready")
        fix_scattered = sem("fix_scattered")

        saved = sems("saved", SETS)
        fall_ready = sem("fall_ready")
        fall_ps = sem("fall_ps")
        flag_ready = sem("flag_ready")
        any_start = sem("any_start")
        any_zeroed = sem("any_zeroed")
        any_cleared = sem("any_cleared")
        any_loaded = sem("any_loaded")
        any_dst_ready = sem("any_dst_ready")
        any_dst_ps = sem("any_dst_ps")
        any_same_step = sem("any_same_step")
        any_same_ready = sem("any_same_ready")
        any_sum_ps = sem("any_sum_ps")
        any_got = sem("any_got")
        any_new = sem("any_new")
        any_put_done = sem("any_put_done")
        all_idx_ready = sem("all_idx_ready")
        all_got = sem("all_got")
        all_step = sem("all_step")
        all_scale = sem("all_scale")
        all_ready = sem("all_ready")
        all_written = sem("all_written")

        block = ctx.enter_context(nc.Block())

        def wait(eng, semaphore, value):
            if not (isinstance(value, int) and value <= 0):
                eng.wait_ge(semaphore, value)

        def slots_in(it, slots):
            return [u for u in slots if not isinstance(it, int) or it * SLOTS + u < CHUNKS]

        def half(h):
            return range(h * TRIO, (h + 1) * TRIO)

        def act_rows(it, u):
            return LAST_ACT_ROWS if isinstance(it, int) and it == ITERS else ACT_ROWS[u]

        def every_quarter(eng, quarter):
            for s in range(SETS):
                quarter(0, s, **QUARTERS[s])
            with eng.Fori(1, ITERS) as it:
                for s in range(SETS):
                    quarter(it, s, **QUARTERS[s])
            for g in LAST_GROUPS:
                quarter(g // SETS, g % SETS, **LAST_QUARTERS[g - LAST_GROUPS[0]])

        def more(it, s, ahead):
            return not isinstance(it, int) or it * SETS + s + ahead < GROUPS

        attr_rows = attr.rearrange("(p t) f -> p t f", p=P)
        x_main = x[0:PER * P].rearrange("(p r) f -> p r f", p=P)
        out_main = out[0:PER * P].rearrange("(p r) f -> p r f", p=P)

        def chunk_of(view, c):
            return view[:, bass.ds(c * ROWS, ROWS), :]

        def tiles_of(t, g, n=G):
            return t[:, bass.ds(g * G, n)]

        @block.sync
        def _(sp):
            for dst, source in ((src_idx[:], src), (dst_win[:], dstw), (logit_lin[:], conf)):
                sp.dma_start(dst, source).then_inc(edges_in, 16)
            consts = [
                (w1[:], W1.rearrange("(c k) o -> k c o", c=3)),
                (b1_col[:], b1.rearrange("(o u) -> o u", u=1)),
                (w2x[:, 0:F], W2),
                (b2x[0:1, 0:F], b2.rearrange("(u o) -> u o", u=1)),
                (b2_col[:], b2.rearrange("(o u) -> o u", u=1)),
                (wa_col[:], Wa[0:F, :]),
                (wa_conf[:], Wa[F:F + 1, :].partition_broadcast(P)),
                (ba_one[:], ba.rearrange("(u o) -> u o", u=1)),
            ]
            for dst, source in consts:
                sp.dma_start(dst, source).then_inc(consts_in, 16)

            sp.dma_start(rest_in[:], x[PER * P:N, :].rearrange("(p r) f -> p r f", p=REST_P)
                         ).then_inc(rest_landed, 16)
            for u in half(0):
                sp.dma_start(nodes[:, u], chunk_of(x_main, u)).then_inc(x_landed[u], 16)
                sp.dma_start(attr_in[:, u], tiles_of(attr_rows, u)).then_inc(attr_landed[u], 16)
            sp.dma_start(attr_in[:, TRIO], tiles_of(attr_rows, TRIO)).then_inc(attr_landed[TRIO], 16)
            sp.wait_ge(flag_ready, 1)
            sp.wait_ge(rest_normed, 1)
            sp.dma_start(out[PER * P:N, :].rearrange("(p r) f -> p r f", p=REST_P), rest_in[:]
                         ).then_inc(rest_stored, 16)

            def load_nodes(c, u):
                sp.dma_start(nodes[:, u], chunk_of(x_main, c)).then_inc(x_landed[u], 16)

            def load_attr(g, s):
                sp.dma_start(attr_in[:, s], tiles_of(attr_rows, g)).then_inc(attr_landed[s], 16)

            def store_nodes(c, u, it):
                sp.wait_ge(act_normed[u], it + 1)
                sp.wait_ge(dve_normed[u], it + 1)
                sp.dma_start(chunk_of(out_main, c), nodes[:, u]).then_inc(stored[u], 16)

            is_unsorted = sp.value_load(unsorted[0:1, 0:1], min_val=0, max_val=1)

            def save_messages(it, s):
                with sp.If(is_unsorted > 0):
                    sp.wait_ge(gated_ready, G * (it * SETS + s + 1))
                    sp.dma_start(tiles_of(messages, it * SETS + s), gated[:, s]).then_inc(saved[s], 16)
                with sp.Else():
                    sp.sem_inc(saved[s], 16)

            def quarter(it, s, load=None, late_store=(), store=(), **_):
                if more(it, s, SETS):
                    sp.wait_ge(turned_ps_ready, 3 * (it * SETS + s + 1))
                    load_attr((it + 1) * SETS + s, s)
                save_messages(it, s)
                to = it + 1 if load == 0 else it
                ahead = list(slots_in(to, half(load))) if load is not None else []

                def load_slots(some):
                    for u in some:
                        wait(sp, stored[u], 16 * to)
                        load_nodes(to * SLOTS + u, u)

                load_slots(ahead[:-1])
                for u in late_store:
                    if not isinstance(it, int) or it:
                        store_nodes((it - 1) * SLOTS + u, u, it - 1)
                for u in slots_in(it, store):
                    store_nodes(it * SLOTS + u, u, it)
                load_slots(ahead[-1:])

            every_quarter(sp, quarter)

            def sort_out(sp):
                sp.wait_ge(any_start, 1)
                sp.wait_ge(any_zeroed, 1)
                zeros = nodes[:, SLOTS - 1]
                sums_main = sums_by_node[0:PER * P].rearrange("(p r) f -> p r f", p=P)
                with sp.Fori(0, CHUNKS) as c:
                    sp.dma_start(chunk_of(sums_main, c), zeros).then_inc(any_cleared, 16)
                sp.dma_start(sums_by_node[PER * P:N, :].rearrange("(p r) f -> p r f", p=REST_P),
                             nodes[0:REST_P, SLOTS - 1, 0:REST_R, :]).then_inc(any_cleared, 16)
                with sp.Fori(1, T + 1) as nth:
                    sp.wait_ge(any_start, nth)
                    sp.dma_start(gated[:, 0, 0, :], messages[:, bass.ds(nth - 1, 1), :].rearrange("p u f -> p (u f)")
                                 ).then_inc(any_loaded, 16)

            with sp.If(is_unsorted > 0):
                sort_out(sp)
            sp.nop()

        @block.gpsimd
        def _(pool):
            pool.memset(ident[:], 0.0).then_inc(pool_const, 1)
            pool.memset(head[:], 0.0).then_inc(pool_const, 1)
            pool.memset(acc[:], 0.0).then_inc(pool_const, 1)
            pool.memset(upper[:], 1.0).then_inc(pool_const, 1)
            pool.memset(ones_all[:], 1.0).then_inc(pool_const, 1)
            pool.wait_ge(pool_const, 5)
            pool.affine_select(out=upper[:], in_=upper[:], compare_op=ALU.is_gt, fill=0.0, base=0,
                               pattern=[[1, P]], channel_multiplier=-1).then_inc(pool_const, 1)
            pool.affine_select(out=ident[:], in_=ident[:], compare_op=ALU.not_equal, fill=1.0, base=0,
                               pattern=[[-1, P]], channel_multiplier=1).then_inc(pool_const, 1)

            def gather(nth, s):
                pool.wait_ge(pool_const, 7)
                pool.wait_ge(idx_ready[s], nth)
                pool.wait_ge(src_free[s], nth)
                for j in range(2 * G):
                    if j == G:
                        pool.wait_ge(pool_const, 7)
                        pool.wait_ge(rows_free[s], nth)
                    pool.indirect_dma_start(
                        out=rows[:, s, j, :], out_offset=None, in_=x[:, :],
                        in_offset=bass.IndirectOffsetOnAxis(ap=idx_slot[:, s, j:j + 1], axis=0),
                    ).then_inc(gathered[s], 16)

            for s in range(SETS):
                pool.sem_inc(src_free[s], 1)
                pool.sem_inc(rows_free[s], 1)
            with pool.Fori(1, ITERS + 1) as nth:
                for s in range(SETS):
                    gather(nth, s)
            for g in LAST_GROUPS:
                gather(g // SETS + 1, g % SETS)
            pool.wait_ge(fix_idx_ready, 1)
            pool.indirect_dma_start(
                out=fix_rows[:, :], out_offset=None, in_=x[:, :],
                in_offset=bass.IndirectOffsetOnAxis(ap=fix_idx[:, 0:1], axis=0),
            ).then_inc(fix_gathered, 16)

            for u in range(SLOTS):
                pool.wait_ge(stored[u], 16 * len(range(u, CHUNKS, SLOTS)))
            pool.wait_ge(rest_stored, 16)

            def scatter(nth, s):
                pool.wait_ge(pool_const, 7)
                pool.wait_ge(out_ready[s], nth)
                pool.wait_ge(ridx_ready[s], nth)
                for j in range(G):
                    pool.indirect_dma_start(
                        out=out[:, :], out_offset=bass.IndirectOffsetOnAxis(ap=ridx_slot[:, s, j:j + 1], axis=0),
                        in_=nodes[:, s, j, :], in_offset=None, bounds_check=N - 1, oob_is_err=False,
                    ).then_inc(scattered[s], 16)

            with pool.Fori(1, GROUPS // SETS + 1) as nth:
                for s in range(SETS):
                    scatter(nth, s)
            for g in range(GROUPS // SETS * SETS, GROUPS):
                scatter(g // SETS + 1, g % SETS)
            pool.wait_ge(fix_ready, 1)
            pool.indirect_dma_start(
                out=out[:, :], out_offset=bass.IndirectOffsetOnAxis(ap=fix_idx[:, 1:2], axis=0),
                in_=fix_out[:, :], in_offset=None, bounds_check=N - 1, oob_is_err=False,
            ).then_inc(fix_scattered, 16)
            for s in range(SETS):
                pool.wait_ge(scattered[s], 16 * G * len(range(s, GROUPS, SETS)))
            pool.wait_ge(fix_scattered, 16)

            def get(to, table, idx, semaphore):
                pool.indirect_dma_start(
                    out=to, out_offset=None, in_=table[:, :],
                    in_offset=bass.IndirectOffsetOnAxis(ap=idx, axis=0)).then_inc(semaphore, 16)

            def put(table, idx, rows_, semaphore):
                pool.indirect_dma_start(
                    out=table[:, :], out_offset=bass.IndirectOffsetOnAxis(ap=idx, axis=0),
                    in_=rows_, in_offset=None, bounds_check=N - 1, oob_is_err=False).then_inc(semaphore, 16)

            def sort_out():
                for s in range(SETS):
                    pool.wait_ge(saved[s], 16 * len(range(s, GROUPS, SETS)))
                pool.sem_inc(any_start, 1)
                pool.wait_ge(any_cleared, 16 * (CHUNKS + 1))
                with pool.Fori(1, T + 1) as nth:
                    pool.wait_ge(pool_const, 7)
                    pool.wait_ge(any_same_ready, nth)
                    get(rows[:, 0, 0, :], sums_by_node, any_get[:, 0:1], any_got)
                    pool.wait_ge(pool_const, 7)
                    pool.wait_ge(any_new, nth)
                    put(sums_by_node, any_put[:, 0:1], rows[:, 0, 1, :], any_put_done)
                    pool.wait_ge(any_put_done, nth * 16)
                    pool.sem_inc(any_start, 1)
                with pool.Fori(1, T + 1) as nth:
                    pool.wait_ge(pool_const, 7)
                    pool.wait_ge(all_idx_ready, nth)
                    get(rows[:, 0, 0, :], sums_by_node, any_get[:, 0:1], all_got)
                    get(rows[:, 0, 1, :], x, any_get[:, 0:1], all_got)
                    pool.wait_ge(pool_const, 7)
                    pool.wait_ge(all_ready, nth)
                    put(out, any_put[:, 0:1], rows[:, 0, 3, :], all_written)
                pool.wait_ge(all_written, 16 * T)

            pool.wait_ge(flag_ready, 1)
            with pool.If(pool.value_load(unsorted[0:1, 0:1], min_val=0, max_val=1) > 0):
                sort_out()
            pool.nop()

        @block.scalar
        def _(act):
            def turn(it, s):
                g = it * SETS + s
                for c in range(3):
                    act.wait_ge(turned_ps_ready, 3 * g + c + 1)
                    if c == 0:
                        wait(act, hid_ps_ready, g - 1)
                    act.activation(turned[:, s % 2, c], turn_ps[:, c], ACT.Copy).then_inc(turned_ready, 1)

            def relu(it, s):
                g = it * SETS + s
                act.wait_ge(hid_ps_ready, g + 1)
                wait(act, msg_ready, g - 1)
                act.activation(hid[:, s % 2], hid_ps[:], ACT.Relu, bias=b1_col[:, 0:1]).then_inc(hid_ready, 1)

            def gates(it, s):
                g = it * SETS + s
                act.wait_ge(msg_ready, g + 1)
                wait(act, gated_ready, G * g)
                act.activation(weight[:].rearrange("p (a b) -> p a b", a=2), msg_ps[:, :, F:512:256],
                               ACT.Sigmoid).then_inc(weight_ready, 1)
                act.wait_ge(weight_ready, g + 1)
                act.wait_ge(rows_free[s], it + 1)
                wait(act, saved[s], 16 * it)
                for j in range(G):
                    act.activation(gated[:, s, j, :], msg(j)[:, 0:F], ACT.Copy,
                                   scale=weight[:, j:j + 1]).then_inc(gated_ready, 1)

            def norm(it, u):
                h = u // TRIO
                act.wait_ge(scale_ready[h], 2 * (it + 1))
                for r in range(act_rows(it, u)):
                    k = (u % TRIO) * ROWS + r
                    last = act.activation(nodes[:, u, r, :], nodes[:, u, r, :], ACT.Identity,
                                          scale=n_sc[:, h, 6, k:k + 1], bias=n_sc[:, h, 7, k:k + 1])
                last.then_inc(act_normed[u], 1)

            def finish(it, s):
                g = it * SETS + s
                wait(act, scattered[s], 16 * G * it)
                act.wait_ge(e_scale[s // 2], 2 * (it + 1))
                for j in range(G):
                    last = act.activation(nodes[:, s, j, :], stash[:, bass.ds(g * G + j, 1), :].rearrange("p u f -> p (u f)"),
                                          ACT.Identity, scale=e_sc[:, s // 2, 6, s % 2, j:j + 1],
                                          bias=e_sc[:, s // 2, 7, s % 2, j:j + 1])
                last.then_inc(out_ready[s], 1)

            def quarter(it, s, late_before=(), before=(), after=(), first=(), **_):
                relu(it, s)
                if more(it, s, 1):
                    turn(it + (s + 1) // SETS, (s + 1) % SETS)
                finish_first(first[:1])
                for u in late_before:
                    if not isinstance(it, int) or it:
                        norm(it - 1, u)
                for u in slots_in(it, before):
                    norm(it, u)
                gates(it, s)
                for u in slots_in(it, after):
                    norm(it, u)
                finish_first(first[1:])

            def finish_first(some):
                for s in some:
                    act.wait_ge(stored[s], 16 * len(range(s, CHUNKS, SLOTS)))
                    finish(0, s)

            act.wait_ge(consts_in, 16 * 8)
            turn(0, 0)
            every_quarter(act, quarter)
            with act.Fori(1, GROUPS // SETS) as it:
                for s in range(SETS):
                    finish(it, s)
            for g in range(GROUPS // SETS * SETS, GROUPS):
                finish(g // SETS, g % SETS)

        @block.tensor
        def _(pe):
            pe.wait_ge(pool_const, 7)
            pe.wait_ge(fall_ready, 2)
            pe.matmul(hid_ps[0:1, P:2 * P], head_len[:], ident[:], start=True, stop=True)
            pe.matmul(hid_ps[:, 0:1], ones_all[:], fall_sum[:], start=True, stop=True).then_inc(fall_ps, 1)
            pe.wait_ge(consts_in, 16 * 8)
            pe.wait_ge(flag_ready, 1)
            pe.transpose(misc_ps[:, 0:P], w2x[:, 0:F], ident[:]).then_inc(w2_in_ps, 1)
            pe.wait_ge(w2_turned_ok, 1)
            pe.matmul(misc_ps[:, 256:257], w2_turned[:], wa_col[:], start=True, stop=True)
            pe.matmul(misc_ps[0:1, 260:261], b2_col[:], wa_col[:], start=True, stop=True).then_inc(wa_in_ps, 1)

            def turn(it, s):
                g = it * SETS + s
                pe.wait_ge(gathered[s], 16 * 2 * G * (it + 1))
                pe.wait_ge(attr_landed[s], 16 * (it + 1))
                wait(pe, turned_ready, 3 * g)
                for c in range(3):
                    for j in range(G):
                        tile = attr_in[:, s, j, :] if c == 2 else rows[:, s, c * G + j, :]
                        last = pe.transpose(turn_ps[:, c, j * P:(j + 1) * P], tile, ident[:])
                        if (c, j) == (1, 0):
                            last.then_inc(src_free[s], 1)
                    last.then_inc(turned_ps_ready, 1)

            def quarter(it, s, **_):
                g = it * SETS + s
                pe.wait_ge(turned_ready, 3 * g + 3)
                wait(pe, hid_ready, g)
                for c in range(3):
                    last = pe.matmul(hid_ps[:], w1[:, c, :], turned[:, s % 2, c, :], start=(c == 0), stop=(c == 2))
                last.then_inc(hid_ps_ready, 1)
                if more(it, s, 1):
                    turn(it + (s + 1) // SETS, (s + 1) % SETS)
                pe.wait_ge(hid_ready, g + 1)
                wait(pe, gated_ready, G * g)
                for j in range(G):
                    pe.matmul(msg(j), hid[:, s % 2, j * P:(j + 1) * P], w2x[:], start=True, stop=False)
                    pe.matmul(msg(j), ones_all[0:1, :], b2x[:], start=False, stop=False)
                    last = pe.matmul(msg(j)[:, F:F + 1], ident[:], logit_lin[:, bass.ds(g * G + j, 1)],
                                     start=False, stop=True)
                last.then_inc(msg_ready, 1)

            turn(0, 0)
            pe.wait_ge(w2_ready, 2)
            pe.wait_ge(lin_ready, 1)
            every_quarter(pe, quarter)

            pe.wait_ge(prep, 1)
            pe.matmul(misc_ps[:, 0:P], dst_f[:, 1:2].to_broadcast([P, P]), ident[:], start=True,
                      stop=True).then_inc(first_ps, 1)
            pe.wait_ge(match_ready, 1)
            lg = LAST_GROUPS[-1]
            pe.wait_ge(edge_step, ESTEPS * (lg + 1))
            pe.matmul(misc_ps[:, 0:P], match[:], acc[:, lg % 2, G - 1, :], start=True,
                      stop=True).then_inc(tails_ps, 1)

            def sort_out():
                pe.wait_ge(fix_ready, 1)
                with pe.Fori(1, T + 1) as nth:
                    pe.wait_ge(any_dst_ready, nth)
                    pe.matmul(misc_ps[:, 0:P], any_dst[:, 0:1].to_broadcast([P, P]), ident[:], start=True,
                              stop=True).then_inc(any_dst_ps, 1)
                    pe.wait_ge(any_same_ready, nth)
                    pe.wait_ge(any_loaded, nth * 16)
                    pe.matmul(hid_ps[:, 0:P], match[:], gated[:, 0, 0, :], start=True,
                              stop=True).then_inc(any_sum_ps, 1)

            with pe.If(pe.value_load(unsorted[0:1, 0:1], min_val=0, max_val=1) > 0):
                sort_out()
            pe.nop()

        @block.vector
        def _(dve):
            done = [0]

            def step(ins):
                done[0] += 1
                ins.then_inc(prep, 1)

            def settle():
                dve.wait_ge(prep, done[0])

            dve.wait_ge(edges_in, 16 * 3)
            d, before, after = dst_f[:, 1:T + 1], dst_f[:, 0:T], dst_f[:, 2:T + 2]
            step(dve.tensor_copy(dst_f[:], dst_win[:]))
            step(dve.tensor_copy(gather_idx[:, :, 0:G], src_idx[:].rearrange("p (g j) -> p g j", j=G)))
            settle()
            step(dve.tensor_scalar(gather_idx[:, :, G:2 * G], dst_f[:, 1:T + 1].rearrange("p (g j) -> p g j", j=G),
                                   float(N - 1), None, ALU.min))
            settle()
            for s in range(SETS):
                dve.tensor_copy(idx_slot[:, s], gather_idx[:, s]).then_inc(idx_ready[s], 1)
            step(dve.tensor_tensor(keep[:], d, before, ALU.is_equal))
            step(dve.tensor_scalar(is_head[:], d, dst_f[:, 0:1], None, ALU.is_equal))
            step(dve.tensor_tensor(skip[:], d, after, ALU.is_equal))
            step(dve.tensor_tensor(falls[:], dst_f[:, 0:T + 1], dst_f[:, 1:T + 2], ALU.is_gt))
            settle()
            step(dve.memset(keep[:, 0:1], 0.0))
            dve.tensor_reduce(fall_sum[:], falls[:], AX_X, ALU.add).then_inc(fall_ready, 1)
            dve.tensor_reduce(head_len[:], is_head[:], AX_X, ALU.add).then_inc(fall_ready, 1)
            step(dve.tensor_tensor(skip[:], skip[:], is_head[:], ALU.add))
            dve.wait_ge(fall_ps, 1)
            step(dve.tensor_scalar(fell[:], hid_ps[:, 0:1], 1.0, None, ALU.min))
            step(dve.tensor_reduce(head_most[:, 0:1], hid_ps[0:1, P:2 * P], AX_X, ALU.max))
            settle()
            step(dve.tensor_scalar(head_most[:, 1:2], head_most[:, 0:1], 1.0 / G, 1.0, ALU.mult, ALU.add))
            settle()
            dve.tensor_scalar(head_count[:], head_most[:, 1:2], float(SETS), float(GROUPS), ALU.max, ALU.min
                              ).then_inc(head_groups_ready, 1)
            dve.tensor_copy(unsorted[:], fell[0:1, :]).then_inc(flag_ready, 1)
            step(dve.tensor_scalar(skip[:], skip[:], fell[:, 0:1], None, ALU.add))
            settle()
            step(dve.scalar_tensor_tensor(row_idx[:], skip[:], float(FAR), d, ALU.mult, ALU.add))
            first, last_, prev, nxt = dst_f[:, 1:2], dst_f[:, T:T + 1], dst_f[:, 0:1], dst_f[:, T + 1:T + 2]
            step(dve.tensor_tensor(small[:, 0:1], first, prev, ALU.is_equal))
            step(dve.tensor_tensor(small[:, 1:2], first, last_, ALU.is_equal))
            step(dve.tensor_tensor(small[:, 2:3], nxt, last_, ALU.is_equal))
            settle()
            step(dve.tensor_tensor(small[:, 3:4], small[:, 1:2], small[:, 2:3], ALU.mult))
            settle()
            step(dve.tensor_scalar(small[:, 4:5], small[:, 3:4], -1.0, 1.0, ALU.mult, ALU.add))
            settle()
            step(dve.tensor_tensor(small[:, 5:6], small[:, 4:5], small[:, 0:1], ALU.mult))
            settle()
            step(dve.tensor_tensor(small[:, 5:6], small[:, 5:6], fell[:], ALU.is_gt))
            settle()
            step(dve.tensor_scalar(small[:, 6:7], small[:, 5:6], -float(FAR), float(FAR), ALU.mult, ALU.add))
            settle()
            step(dve.tensor_tensor(fix_idx[:, 1:2], small[:, 6:7], first, ALU.add))
            settle()
            dve.tensor_copy(fix_idx[:, 0:1], first).then_inc(fix_idx_ready, 1)
            dve.wait_ge(consts_in, 16 * 8)
            dve.tensor_scalar(logit_lin[:], logit_lin[:], wa_conf[:, 0:1], None, ALU.mult).then_inc(lin_ready, 1)
            dve.wait_ge(w2_in_ps, 1)
            dve.tensor_copy(w2_turned[:], misc_ps[:, 0:P]).then_inc(w2_turned_ok, 1)
            dve.wait_ge(wa_in_ps, 1)
            dve.tensor_copy(w2x[:, F:F + 1], misc_ps[:, 256:257]).then_inc(w2_ready, 1)
            dve.tensor_tensor(b2x[0:1, F:F + 1], misc_ps[0:1, 260:261], ba_one[:], ALU.add).then_inc(w2_ready, 1)
            settle()
            dve.wait_ge(pool_const, 7)

            def scales(st, sc, sem_, base, final):
                mean_e, m2_e, mean_o, m2_o = (st[:, :, k] for k in (1, 2, 4, 5))
                mean2, apart, v, y, a = (sc[:, k] for k in range(5))
                n = [0]

                def then(ins, wait=True):
                    n[0] += 1
                    ins.then_inc(sem_, 1)
                    if wait:
                        dve.wait_ge(sem_, base + n[0])

                then(dve.tensor_tensor(mean2, mean_e, mean_o, ALU.add), False)
                then(dve.tensor_tensor(apart, mean_e, mean_o, ALU.subtract), False)
                then(dve.tensor_tensor(v, m2_e, m2_o, ALU.add))
                then(dve.scalar_tensor_tensor(a, apart, F / 4.0, apart, ALU.mult, ALU.mult))
                then(dve.scalar_tensor_tensor(v, v, F * EPS, a, ALU.add, ALU.add))
                then(dve.tensor_scalar(y.bitcast(I32), v.bitcast(I32), -0.5, float(RSQRT_BITS), ALU.mult, ALU.add))
                then(dve.tensor_tensor(a, y, y, ALU.mult))
                then(dve.tensor_tensor(a, a, v, ALU.mult))
                then(dve.scalar_tensor_tensor(a, a, -10 / 3, a, ALU.add, ALU.mult))
                then(dve.scalar_tensor_tensor(y, a, 5.0, y, ALU.add, ALU.mult))
                then(dve.tensor_tensor(a, y, y, ALU.mult))
                then(dve.tensor_tensor(a, a, v, ALU.mult))
                then(dve.scalar_tensor_tensor(y, a, -3 * (8 / 3) ** 2, y, ALU.add, ALU.mult))
                unit = -ROOT * (3 / 8) * (9 / 128)
                dve.tensor_scalar(sc[:, 6], y, unit, None, ALU.mult).then_inc(final, 1)
                dve.scalar_tensor_tensor(sc[:, 7], mean2, -0.5 * unit, y, ALU.mult, ALU.mult).then_inc(final, 1)
                assert n[0] == SSTEPS

            def stat_rows(it, slots):
                return [(stat_row, it, u, r) for u in slots_in(it, slots) for r in range(ROWS)]

            def norm_rows(it, slots):
                return [(norm_row, it, u, r) for u in slots_in(it, slots) for r in range(act_rows(it, u), ROWS)]

            def do(some):
                for row, it, u, r in some:
                    row(it, u, r)

            def stat_row(it, u, r):
                if r == 0:
                    dve.wait_ge(x_landed[u], 16 * (it + 1))
                ins = dve.bn_stats(n_stats[:, (u % TRIO) * ROWS + r, :], nodes[:, u, r, :])
                if r == ROWS - 1:
                    ins.then_inc(node_stat, 1)

            def norm_row(it, u, r):
                h = u // TRIO
                if r == act_rows(it, u):
                    dve.wait_ge(scale_ready[h], 2 * (it + 1))
                k = (u % TRIO) * ROWS + r
                ins = dve.tensor_scalar(nodes[:, u, r, :], nodes[:, u, r, :], n_sc[:, h, 6, k:k + 1],
                                        n_sc[:, h, 7, k:k + 1], ALU.mult, ALU.add)
                if r == ROWS - 1:
                    ins.then_inc(dve_normed[u], 1)

            def node_scales(it, h):
                n = len(slots_in(it, half(h)))
                before = min(CHUNKS, it * SLOTS + h * TRIO) if isinstance(it, int) else it * SLOTS + h * TRIO
                dve.wait_ge(node_stat, before + n)
                scales(n_stats[:, 0:n * ROWS], n_sc[:, h, :, 0:n * ROWS], node_step, SSTEPS * (2 * it + h),
                       scale_ready[h])

            def next_indices(it, s):
                dve.wait_ge(gathered[s], 16 * 2 * G * (it + 1))
                dve.tensor_copy(idx_slot[:, s], gather_idx[:, bass.ds((it + 1) * SETS + s, 1), :]
                                .rearrange("p u j -> p (u j)")).then_inc(idx_ready[s], 1)

            def heads(it, s):
                for j in range(G):
                    t = (it * SETS + s) * G + j
                    dve.wait_ge(gated_ready, t + 1)
                    wait(dve, head_step, t)
                    dve.scalar_tensor_tensor(head[:], gated[:, s, j, :], is_head[:, bass.ds(t, 1)],
                                             head[:], ALU.mult, ALU.add).then_inc(head_step, 1)

            dve.wait_ge(head_groups_ready, 1)
            head_groups = dve.value_load(head_count[0:1, 0:1], min_val=SETS, max_val=GROUPS)

            def sums(it, s, rows_beside):
                g = it * SETS + s
                base = ESTEPS * g
                b = s % 2
                if isinstance(it, int) and it == 0:
                    heads(it, s)
                else:
                    with dve.If(head_groups > g):
                        heads(it, s)
                wait(dve, edge_step, base)
                for j in range(G):
                    t = g * G + j
                    prev_acc = acc[:, b, j - 1, :] if j else acc[:, 1 - b, G - 1, :]
                    dve.wait_ge(gated_ready, t + 1)
                    if j:
                        dve.wait_ge(edge_step, base + j)
                    dve.scalar_tensor_tensor(acc[:, b, j, :], prev_acc, keep[:, bass.ds(t, 1)],
                                             gated[:, s, j, :], ALU.mult, ALU.add).then_inc(edge_step, 1)
                    do(rows_beside[len(rows_beside) * j // G:len(rows_beside) * (j + 1) // G])
                dve.wait_ge(edge_step, base + G)
                dve.tensor_tensor(tiles_of(stash, g), acc[:, b], rows[:, s, G:2 * G, :], ALU.add
                                  ).then_inc(rows_free[s], 1)

            def finish(it, pair, n=2):
                slots = range(2 * pair, 2 * pair + n)
                for k, s in enumerate(slots):
                    wait(dve, scattered[s], 16 * G * it)
                    dve.tensor_copy(ridx_slot[:, s], tiles_of(row_idx, it * SETS + s)).then_inc(ridx_ready[s], 1)
                    dve.wait_ge(rows_free[s], it + 2)
                    for j in range(G):
                        tile = stash[:, bass.ds((it * SETS + s) * G + j, 1), :].rearrange("p u f -> p (u f)")
                        last = dve.bn_stats(e_stats[:, k, j, :], tile)
                last.then_inc(e_stat, 1)
                dve.wait_ge(e_stat, 2 * it + pair + 1)
                for s in slots:
                    wait(dve, out_ready[s], it)
                scales(e_stats[:, 0:n].rearrange("p k g w -> p (k g) w"),
                       e_sc[:, pair, :, 0:n].rearrange("p w k g -> p w (k g)"), final_step,
                       SSTEPS * (2 * it + pair), e_scale[pair])

            def last_nodes():
                dve.wait_ge(rest_landed, 16)
                for r in range(REST_R):
                    last = dve.bn_stats(rest_stats[:, r, :], rest_in[:, r, :])
                last.then_inc(rest_step, 1)
                dve.wait_ge(rest_step, 1)
                scales(rest_stats[:], rest_sc[:], rest_step, 1, rest_scale)
                dve.wait_ge(rest_scale, 2)
                for r in range(REST_R):
                    last = dve.tensor_scalar(rest_in[:, r, :], rest_in[:, r, :], rest_sc[:, 6, r:r + 1],
                                             rest_sc[:, 7, r:r + 1], ALU.mult, ALU.add)
                last.then_inc(rest_normed, 1)

            def quarter(it, s, stats=(), scale=None, norm=None, first_scales=None, **_):
                if more(it, s, SETS):
                    next_indices(it, s)
                rows_now = (norm_rows(it, half(norm)) if norm is not None else []) + stat_rows(it, stats)
                group = it * SETS + s
                if isinstance(group, int) and group == 0:
                    do(rows_now)
                else:
                    first_beside = max(0, len(rows_now) - BESIDE)
                    do(rows_now[:first_beside])
                    sums(*((it, s - 1) if s else (it - 1, SETS - 1)), rows_now[first_beside:])
                if scale is not None:
                    node_scales(it, scale)
                if first_scales is not None:
                    finish(0, first_scales)

            last_nodes()
            every_quarter(dve, quarter)
            sums(LAST_GROUPS[-1] // SETS, LAST_GROUPS[-1] % SETS, [])

            with dve.Fori(1, GROUPS // SETS) as it:
                for pair in range(SETS // 2):
                    finish(it, pair)

            dve.wait_ge(first_ps, 1)
            dve.tensor_scalar(match[:], misc_ps[:, 0:P], last_, None, ALU.is_equal).then_inc(fix_step, 1)
            dve.wait_ge(fix_step, 1)
            dve.tensor_tensor(match[:], match[:], upper[:], ALU.mult).then_inc(match_ready, 1)
            dve.wait_ge(fix_gathered, 16)
            dve.wait_ge(head_step, head_groups * G)
            dve.tensor_tensor(fix_rows[:], fix_rows[:], head[:], ALU.add).then_inc(fix_step, 1)
            dve.wait_ge(fix_step, 2)
            dve.wait_ge(tails_ps, 1)
            dve.tensor_tensor(fix_rows[:], fix_rows[:], misc_ps[:, 0:P], ALU.add).then_inc(fix_step, 1)
            dve.wait_ge(fix_step, 3)
            dve.bn_stats(r_stats[:, :], fix_rows[:, :]).then_inc(rest_step, 1)
            dve.wait_ge(rest_step, SSTEPS + 2)
            scales(r_stats[:].rearrange("p (u k) -> p u k", u=1), r_sc[:], rest_step, SSTEPS + 2, rest_scale)
            dve.wait_ge(rest_scale, 4)
            dve.tensor_scalar(fix_out[:], fix_rows[:], r_sc[:, 6, :], r_sc[:, 7, :],
                              ALU.mult, ALU.add).then_inc(fix_ready, 1)

            finish(GROUPS // SETS, 0, GROUPS % SETS)

            def sort_out():
                dve.wait_ge(any_start, 1)
                dve.memset(nodes[:, SLOTS - 1], 0.0).then_inc(any_zeroed, 1)
                with dve.Fori(1, T + 1) as nth:
                    dve.wait_ge(any_start, nth)
                    dst_of = dst_f[:, bass.ds(nth, 1)]
                    dve.tensor_copy(any_dst[:], dst_of).then_inc(any_dst_ready, 1)
                    dve.tensor_scalar(any_get[:], dst_of, float(N - 1), None, ALU.min).then_inc(any_same_step, 1)
                    dve.wait_ge(any_dst_ready, nth)
                    dve.wait_ge(any_dst_ps, nth)
                    dve.tensor_scalar(match[:], misc_ps[:, 0:P], any_dst[:, 0:1], None, ALU.is_equal
                                      ).then_inc(any_same_step, 1)
                    dve.wait_ge(any_same_step, nth * 5 - 3)
                    dve.tensor_tensor(fix_out[:], match[:], upper[:], ALU.mult).then_inc(any_same_step, 1)
                    dve.wait_ge(any_same_step, nth * 5 - 2)
                    dve.tensor_reduce(any_later[:], fix_out[:], AX_X, ALU.add).then_inc(any_same_step, 1)
                    dve.wait_ge(any_same_step, nth * 5 - 1)
                    dve.scalar_tensor_tensor(any_put[:], any_later[:], float(FAR), any_dst[:], ALU.mult, ALU.add
                                             ).then_inc(any_same_step, 1)
                    dve.wait_ge(any_same_step, nth * 5)
                    dve.tensor_copy(row_idx[:, bass.ds(nth - 1, 1)], any_put[:]).then_inc(any_same_ready, 1)
                    dve.wait_ge(any_got, nth * 16)
                    dve.wait_ge(any_sum_ps, nth)
                    dve.tensor_tensor(rows[:, 0, 1, :], rows[:, 0, 0, :], hid_ps[:, 0:P], ALU.add).then_inc(any_new, 1)
                dve.wait_ge(any_start, T + 1)
                with dve.Fori(1, T + 1) as nth:
                    dve.tensor_scalar(any_get[:], dst_f[:, bass.ds(nth, 1)], float(N - 1), None, ALU.min
                                      ).then_inc(all_step, 1)
                    dve.wait_ge(all_step, nth * (SSTEPS + 3) - (SSTEPS + 2))
                    dve.tensor_copy(any_put[:], row_idx[:, bass.ds(nth - 1, 1)]).then_inc(all_idx_ready, 1)
                    dve.wait_ge(all_got, nth * 32)
                    dve.tensor_tensor(rows[:, 0, 2, :], rows[:, 0, 0, :], rows[:, 0, 1, :], ALU.add).then_inc(all_step, 1)
                    dve.wait_ge(all_step, nth * (SSTEPS + 3) - (SSTEPS + 1))
                    dve.bn_stats(r_stats[:], rows[:, 0, 2, :]).then_inc(all_step, 1)
                    dve.wait_ge(all_step, nth * (SSTEPS + 3) - SSTEPS)
                    scales(r_stats[:].rearrange("p (u k) -> p u k", u=1), r_sc[:], all_step,
                           nth * (SSTEPS + 3) - SSTEPS, all_scale)
                    dve.wait_ge(all_scale, nth * 2)
                    dve.tensor_scalar(rows[:, 0, 3, :], rows[:, 0, 2, :], r_sc[:, 6, :], r_sc[:, 7, :],
                                      ALU.mult, ALU.add).then_inc(all_ready, 1)
                    dve.wait_ge(all_written, nth * 16)

            dve.wait_ge(flag_ready, 1)
            with dve.If(dve.value_load(unsorted[0:1, 0:1], min_val=0, max_val=1) > 0):
                sort_out()
            dve.engine_nop()


def kernel(x, src, dst, edge_attr_128, edge_weight1, L0_gnn_W1, L0_gnn_b1, L0_gnn_W2, L0_gnn_b2, L0_gnn_Wa,
           L0_gnn_ba):
    import numpy as np
    import concourse.bacc as bacc
    from concourse.bass_utils import run_bass_kernel_spmd

    N, F = x.shape
    E = src.shape[0]
    T = -(-E // (P * G)) * G
    fill = P * T - E
    dst = np.ascontiguousarray(dst)
    line = np.concatenate([np.full(1, -1, dst.dtype), dst, np.full(fill + 1, N, dst.dtype)])
    arrays = {
        "x": np.ascontiguousarray(x),
        "src": np.concatenate([src, np.zeros(fill, dst.dtype)]).reshape(P, T),
        "dst_window": np.ascontiguousarray(np.lib.stride_tricks.sliding_window_view(line, T + 2)[::T]),
        "edge_attr": np.concatenate([edge_attr_128, np.zeros((fill, F), np.float32)]),
        "edge_weight": np.concatenate([edge_weight1, np.zeros((fill, 1), np.float32)]).reshape(P, T),
        "W1": np.ascontiguousarray(L0_gnn_W1), "b1": np.ascontiguousarray(L0_gnn_b1),
        "W2": np.ascontiguousarray(L0_gnn_W2), "b2": np.ascontiguousarray(L0_gnn_b2),
        "Wa": np.ascontiguousarray(L0_gnn_Wa), "ba": np.ascontiguousarray(L0_gnn_ba),
    }
    nc = bacc.Bacc("TRN2", target_bir_lowering=False, num_devices=1)
    args = [nc.dram_tensor(n, a.shape, mybir.dt.from_np(a.dtype), kind="ExternalInput").ap()
            for n, a in arrays.items()]
    out = nc.dram_tensor("out", (N, F), F32, kind="ExternalOutput").ap()
    build(nc, *args, out)
    r = run_bass_kernel_spmd(nc, [arrays], core_ids=[0])
    return r.results[0]["out"]
```
